# Optimizing a Trainium2 kernel written in Bass

```python
import numpy as np
import jax
import jax.numpy as jnp

def _softmax(x, axis=-1):
    return jax.nn.softmax(x, axis=axis)

def _gelu(x):
    return jax.nn.gelu(x, approximate=True)

def _silu(x):
    return jax.nn.silu(x)

def _sigmoid(x):
    return jax.nn.sigmoid(x)

def _layernorm(x, axis=-1, eps=1e-05):
    m = jnp.mean(x, axis=axis, keepdims=True)
    v = jnp.var(x, axis=axis, keepdims=True)
    return (x - m) / jnp.sqrt(v + eps)

def _scatter_add(tgt, idx, src, axis=0):
    return tgt.at[idx].add(src)

def _segment_sum(src, seg, n):
    return jax.ops.segment_sum(src, seg, n)
kernel_name = 'mk_seq_preln_d1_jaxref_r8_61decb'

def setup_inputs(seed: int=0):
    np.random.seed(seed)
    _w = jnp.asarray

    def _L0_attn_setup():
        import jax, jax.numpy as jnp
        import numpy as np
        import math
        NH, NKV, D = (32, 8, 128)

        def _alibi_slopes(n):
            cp2 = 2 ** math.floor(math.log2(n))
            base = 2.0 ** (-8.0 / cp2)
            slopes = base ** np.arange(1, cp2 + 1, dtype=np.float32)
            if cp2 != n:
                extra_base = 2.0 ** (-4.0 / cp2)
                extra = extra_base ** np.arange(1, 1 + 2 * (n - cp2), 2, dtype=np.float32)
                slopes = np.concatenate([slopes, extra])
            return slopes.astype(np.float32)
        key = jax.random.key(seed)
        k1, k2, k3 = jax.random.split(key, 3)
        B, S, H = (4, 128, 512)
        qkv_out = NH * D + 2 * NKV * D
        return {'hidden_states': jax.random.normal(k1, (B, S, H), jnp.float32) * 0.02, 'w_qkv': jax.random.normal(k2, (H, qkv_out), jnp.float32) * 0.02, 'w_o': jax.random.normal(k3, (NH * D, H), jnp.float32) * 0.02}
    _L0_attn_in = _L0_attn_setup()

    def _L0_ffn_setup():
        import jax, jax.numpy as jnp
        import numpy as np
        IN_F = 512
        OUT_F = 512
        N_CLUSTERS = 64
        THRESHOLD = 0.01
        TEMPERATURE = 0.1
        BATCH, SEQ = (4, 256)
        key = jax.random.key(seed)
        k1, k2, k3, k4, k5 = jax.random.split(key, 5)
        s = 1.0 / np.sqrt(IN_F)
        return {'input': jax.random.normal(k1, (BATCH, SEQ, IN_F), dtype=jnp.float32), 'weight': jax.random.normal(k2, (OUT_F, IN_F), dtype=jnp.float32) * s, 'bias': jax.random.uniform(k3, (OUT_F,), dtype=jnp.float32, minval=-s, maxval=s), 'centroids': jax.random.normal(k4, (N_CLUSTERS, IN_F), dtype=jnp.float32) * s, 'assignments': jax.random.randint(k5, (OUT_F,), 0, N_CLUSTERS, dtype=jnp.int32)}
    _L0_ffn_in = _L0_ffn_setup()
    _d = {'L0_attn_hidden_states': _L0_attn_in['hidden_states'], 'L0_attn_w_qkv': _L0_attn_in['w_qkv'], 'L0_attn_w_o': _L0_attn_in['w_o'], 'L0_ffn_weight': _L0_ffn_in['weight'], 'L0_ffn_bias': _L0_ffn_in['bias'], 'L0_ffn_centroids': _L0_ffn_in['centroids'], 'L0_ffn_assignments': _L0_ffn_in['assignments']}
    _x0 = _d['L0_attn_hidden_states']
    _d['L0_attn_hidden_states'] = jax.random.normal(jax.random.fold_in(jax.random.key(seed), 1), (8, 256, 512), dtype=_x0.dtype)
    del _x0
    return _d

def reference(L0_attn_hidden_states, L0_attn_w_qkv, L0_attn_w_o, L0_ffn_weight, L0_ffn_bias, L0_ffn_centroids, L0_ffn_assignments):

    def _L0_attn_ref(hidden_states, w_qkv, w_o):
        import jax, jax.numpy as jnp
        import numpy as np
        import math
        NH, NKV, D = (32, 8, 128)

        def _alibi_slopes(n):
            cp2 = 2 ** math.floor(math.log2(n))
            base = 2.0 ** (-8.0 / cp2)
            slopes = base ** np.arange(1, cp2 + 1, dtype=np.float32)
            if cp2 != n:
                extra_base = 2.0 ** (-4.0 / cp2)
                extra = extra_base ** np.arange(1, 1 + 2 * (n - cp2), 2, dtype=np.float32)
                slopes = np.concatenate([slopes, extra])
            return slopes.astype(np.float32)
        B, S, H = hidden_states.shape
        G = NH // NKV
        scale = D ** (-0.5)
        qkv = hidden_states @ w_qkv
        q = qkv[..., :NH * D].reshape(B, S, NKV, G, D)
        k = qkv[..., NH * D:NH * D + NKV * D].reshape(B, S, NKV, D)
        v = qkv[..., NH * D + NKV * D:].reshape(B, S, NKV, D)
        scores = jnp.einsum('bqhgd,bkhd->bhgqk', q, k) * scale
        slopes = jnp.asarray(_alibi_slopes(NH)).reshape(NKV, G)
        pos = jnp.arange(S)
        rel = pos[:, None] - pos[None, :]
        sqrt_dist = jnp.sqrt(jnp.maximum(rel, 0).astype(jnp.float32))
        bias = -slopes[:, :, None, None] * sqrt_dist
        bias = jnp.where(rel[None, None] >= 0, bias, -jnp.inf)
        attn = jax.nn.softmax(scores + bias[None], axis=-1)
        out = jnp.einsum('bhgqk,bkhd->bqhgd', attn, v).reshape(B, S, NH * D)
        return out @ w_o

    def _L0_ffn_ref(input, weight, bias, centroids, assignments):
        import jax, jax.numpy as jnp
        import numpy as np
        IN_F = 512
        OUT_F = 512
        N_CLUSTERS = 64
        THRESHOLD = 0.01
        TEMPERATURE = 0.1
        BATCH, SEQ = (4, 256)
        shape = input.shape
        x = input.reshape(-1, shape[-1])
        dots = jax.nn.softmax(x @ centroids.T / TEMPERATURE, axis=-1)
        hits = dots > THRESHOLD
        query_sel = jnp.any(hits, axis=1)
        cluster_sel = jnp.any(hits, axis=0)
        row_sel = cluster_sel[assignments]
        dense = x @ weight.T + bias
        out = jnp.where(query_sel[:, None] & row_sel[None, :], dense, jnp.zeros((), dense.dtype))
        return out.reshape(*shape[:-1], -1)
    x = L0_attn_hidden_states
    x = x + _L0_attn_ref(_layernorm(x, axis=-1), L0_attn_w_qkv, L0_attn_w_o)
    x = x + _L0_ffn_ref(_layernorm(x, axis=-1), L0_ffn_weight, L0_ffn_bias, L0_ffn_centroids, L0_ffn_assignments)
    return x

_drawn_inputs = setup_inputs


def setup_inputs(seed=0):
    import zlib

    import numpy as np

    out = dict(_drawn_inputs(seed))
    spreads = {}
    factors = {'L0_ffn_bias': 3.354}
    for name, (base, spread) in spreads.items():
        noise = np.random.default_rng([zlib.crc32(name.encode()), seed]).standard_normal(out[name].shape)
        drawn = base * np.exp(spread * noise) if base else spread * noise
        out[name] = jnp.asarray(drawn.astype(out[name].dtype))
    for name, factor in factors.items():
        out[name] = (out[name] * factor).astype(out[name].dtype)
    return out
```

```python
from contextlib import ExitStack

import concourse.bass as bass
from concourse import mybir

ALU = mybir.AluOpType
ACT = mybir.ActivationFunctionType
F32 = mybir.dt.float32
F32R = mybir.dt.float32r
BF16 = mybir.dt.bfloat16
I32 = mybir.dt.int32
AX_X = mybir.AxisListType.X

P = 128
BATCH, SEQ, HID = 8, 256, 512
NH, NKV, D = 32, 8, 128
HPG = NH // NKV
TOK = BATCH * SEQ
TILES = TOK // P
NC = HID // P
UT = 512
QUADS = TOK // UT
TPQ = UT // P
UNITS = NKV * QUADS
QKV_W = (HPG + 2) * D
SCALE = float(D) ** -0.5
LN_EPS = 1e-5
MASKED = -3.0e38
BIGGEST = 3.0e38
CLUSTERS = 64
INV_TEMP = 1.0 / 0.10000000149011612
THRESHOLD = 0.01
ALIBI_BASE = 2.0 ** (-8.0 / NH)

PROJ_OUTS = 6
CHUNKS = 6
SCORE_BANKS = 6
QTILES = 4


def build(nc, x_in, w_qkv, w_o, w_ffn, b_ffn, cents, assign, out):
    ctx = ExitStack()
    with ctx:
        def sem(name):
            return ctx.enter_context(nc.semaphore(name))

        def sb(name, shape, dt, where=ctx):
            return where.enter_context(nc.sbuf_tensor(name, shape, dt))

        acc = sb("acc", [P, TILES * HID], F32)
        ident = sb("ident", [P, P], F32)
        stats = sb("stats", [P, TPQ, 6], F32)
        meanvar = sb("meanvar", [P, TPQ, 2], F32)
        rs = sb("rs", [P, 6, TPQ], F32)

        att = ExitStack()
        xnT_hi = sb("xnT_hi", [P, NC, TOK], F32R, att)
        xnT_lo = sb("xnT_lo", [P, NC, TOK], F32R, att)
        wqkv_hi = sb("wqkv_hi", [P, NC, QKV_W], F32R, att)
        wqkv_lo = sb("wqkv_lo", [P, NC, QKV_W], F32R, att)
        wo_hi = sb("wo_hi", [P, HPG, HID], F32R, att)
        wo_lo = sb("wo_lo", [P, HPG, HID], F32R, att)
        raw = sb("raw", [P, 2, QKV_W], F32, att)
        qT_hi = sb("qT_hi", [P, HPG, UT], F32R, att)
        qT_lo = sb("qT_lo", [P, HPG, UT], F32R, att)
        kT_hi = sb("kT_hi", [P, UT], F32R, att)
        kT_lo = sb("kT_lo", [P, UT], F32R, att)
        vT = sb("vT", [P, UT], F32, att)
        v_hi = sb("v_hi", [P, TPQ, D], F32R, att)
        v_lo = sb("v_lo", [P, TPQ, D], F32R, att)
        prob = sb("prob", [P, SCORE_BANKS, 512], F32, att)
        pT_hi = sb("pT_hi", [P, 2, 512], F32R, att)
        pT_lo = sb("pT_lo", [P, 2, 512], F32R, att)
        oT_hi = sb("oT_hi", [P, 3, 512], F32R, att)
        oT_lo = sb("oT_lo", [P, 3, 512], F32R, att)
        bias = sb("bias", [P, HPG, SEQ], F32, att)
        dist = sb("dist", [P, SEQ], F32, att)
        negmax = sb("negmax", [P, 16], F32, att)
        rowsum = sb("rowsum", [P, 16], F32, att)
        rinv = sb("rinv", [P, 16], F32, att)
        att.close()

        ffn = ExitStack()
        x2T_hi = sb("x2T_hi", [P, NC, UT], F32R, ffn)
        x2T_lo = sb("x2T_lo", [P, NC, UT], F32R, ffn)
        wT_hi = sb("wT_hi", [P, NC, HID], F32R, ffn)
        wT_lo = sb("wT_lo", [P, NC, HID], F32R, ffn)
        cT_hi = sb("cT_hi", [P, NC, CLUSTERS], F32R, ffn)
        cT_lo = sb("cT_lo", [P, NC, CLUSTERS], F32R, ffn)
        w_raw = sb("w_raw", [P, NC, HID], F32, ffn)
        c_raw = sb("c_raw", [CLUSTERS, HID], F32, ffn)
        bias_bc = sb("bias_bc", [P, HID], F32, ffn)
        assign_bc = sb("assign_bc", [CLUSTERS, HID], I32, ffn)
        assign_f = sb("assign_f", [CLUSTERS, HID], F32, ffn)
        cluster_id = sb("cluster_id", [CLUSTERS, 1], F32, ffn)
        onehot = sb("onehot", [CLUSTERS, HID], BF16, ffn)
        ones = sb("ones", [P, P], BF16, ffn)
        stage = sb("stage", [P, TPQ, HID], F32, ffn)
        selected = sb("selected", [P, TILES * HID], F32, ffn)
        fbias = sb("fbias", [P, 2, HID], F32, ffn)
        cl_nmax = sb("cl_nmax", [P, TPQ], F32, ffn)
        cl_bias = sb("cl_bias", [P, TPQ], F32, ffn)
        cl_exp = sb("cl_exp", [P, TPQ, CLUSTERS], F32, ffn)
        cl_sum = sb("cl_sum", [P, TPQ], F32, ffn)
        cl_rinv = sb("cl_rinv", [P, TPQ], F32, ffn)
        cl_prob = sb("cl_prob", [P, TPQ, CLUSTERS], F32, ffn)
        hits = sb("hits", [P, TILES * CLUSTERS], F32, ffn)
        query_sel = sb("query_sel", [P, TPQ], F32, ffn)
        any_hit = sb("any_hit", [P, CLUSTERS], BF16, ffn)
        cluster_sel = sb("cluster_sel", [CLUSTERS, P], BF16, ffn)
        ffn.close()

        ps = ctx.enter_context(nc.psum_tensor("ps", [P, 8, 512], F32))
        PJ = (0, 1)
        TR = (2, 3)
        PV = (4, 5)
        SC = (6, 7)

        x_loaded = [sem(f"x_loaded{q}") for q in range(QUADS)]
        raw_loaded = [sem("raw_loaded0"), sem("raw_loaded1")]
        ffn_loaded = sem("ffn_loaded")
        stored = sem("stored")
        pool_step = sem("pool_step")
        pool_marks = sem("pool_marks")
        ident_ready = sem("ident_ready")
        dist_sq = sem("dist_sq")
        raw_split = sem("raw_split")
        wqkv_ready = sem("wqkv_ready")
        wo_ready = sem("wo_ready")
        bias_ready = sem("bias_ready")
        ffn_consts = sem("ffn_consts")
        xn_mm = sem("xn_mm")
        qkv_mm = sem("qkv_mm")
        pT_mm = sem("pT_mm")
        pv_mm = sem("pv_mm")
        wo_mm = sem("wo_mm")
        s_mm = sem("s_mm")
        v_mm = sem("v_mm")
        wT_mm = sem("wT_mm")
        x2_mm = sem("x2_mm")
        logit_mm = sem("logit_mm")
        dense_mm = sem("dense_mm")
        sel_mm = sem("sel_mm")
        dist_sqrt = sem("dist_sqrt")
        std_ready = sem("std_ready")
        xnT_hi_done = sem("xnT_hi_done")
        qkv_hi_done = sem("qkv_hi_done")
        pT_hi_done = sem("pT_hi_done")
        oT_hi_done = sem("oT_hi_done")
        exp_done = sem("exp_done")
        v_hi_done = sem("v_hi_done")
        wT_hi_done = sem("wT_hi_done")
        x2T_hi_done = sem("x2T_hi_done")
        cl_exp_done = sem("cl_exp_done")
        dve_step = sem("dve_step")
        dist_ready = sem("dist_ready")
        var_ready = sem("var_ready")
        xn_ready = sem("xn_ready")
        xnT_lo_done = sem("xnT_lo_done")
        qk_lo_done = sem("qk_lo_done")
        pT_lo_done = sem("pT_lo_done")
        oT_lo_done = sem("oT_lo_done")
        scores_biased = sem("scores_biased")
        dve_marks = sem("dve_marks")
        rinv_done = sem("rinv_done")
        probs_ready = sem("probs_ready")
        v_lo_done = sem("v_lo_done")
        added = sem("added")
        wT_lo_done = sem("wT_lo_done")
        x2_ready = sem("x2_ready")
        x2T_lo_done = sem("x2T_lo_done")
        cl_max_done = sem("cl_max_done")
        hits_done = sem("hits_done")
        dense_out = sem("dense_out")
        any_ready = sem("any_ready")
        csel_ready = sem("csel_ready")
        final = sem("final")

        block = ctx.enter_context(nc.Block())

        def group_count(u):
            return (u + QUADS) >> 2

        def quad_of(u):
            return u % QUADS

        def score_slices(i):
            b, part = i // 3, i % 3
            if part == 0:
                return b, 0, [(h, h * P, 0, P, 8 * b + h) for h in range(HPG)]
            return b, 1, [(h, (h % 2) * SEQ, 0, SEQ, 8 * b + 2 + h + (2 if part else 0)) for h in (2 * part - 2, 2 * part - 1)]

        def stat_cols(i):
            b, part = i // 3, i % 3
            first = 8 * b + (0, 4, 6)[part]
            return first, first + (4 if part == 0 else 2)

        def chunk_blocks(c):
            b, part = c // 3, c % 3
            if part == 0:
                return b, 0, 0, [(3 * b, h * P) for h in range(HPG)]
            kt = part - 1
            return b, 1, kt, [(3 * b + 1 + h // 2, (h % 2) * SEQ + kt * P) for h in range(HPG)]

        @block.sync
        def _(sp):
            def load_qkv(g, c):
                rows = w_qkv[c * P:(c + 1) * P, :]
                slot = raw[:, c % 2, :]
                done = raw_loaded[c % 2]
                sp.dma_start(slot[:, 0:HPG * D], rows[:, bass.ds(g * (HPG * D), HPG * D)]).then_inc(done, 16)
                sp.dma_start(slot[:, HPG * D:HPG * D + D], rows[:, bass.ds(g * D + NH * D, D)]).then_inc(done, 16)
                sp.dma_start(slot[:, HPG * D + D:QKV_W], rows[:, bass.ds(g * D + (NH + NKV) * D, D)]).then_inc(done, 16)

            def load_o(g, h):
                rows = w_o[bass.ds(g * (HPG * D) + h * D, D), :]
                sp.dma_start(raw[:, h % 2, 0:HID], rows).then_inc(raw_loaded[h % 2], 16)

            def load_group(g, first):
                for n in range(2 * NC):
                    if not (first and n < 2):
                        sp.wait_ge(raw_split, g * (2 * NC) + n - 1)
                    load_qkv(g, n) if n < NC else load_o(g, n - NC)

            sp.dma_start(acc[:, 0:TPQ * HID].rearrange("p (t d) -> p t d", t=TPQ),
                         x_in[0:UT, :].rearrange("(t p) d -> p t d", p=P)).then_inc(x_loaded[0], 16)
            load_qkv(0, 0)
            load_qkv(0, 1)
            for q in range(1, QUADS):
                sp.dma_start(acc[:, q * TPQ * HID:(q + 1) * TPQ * HID].rearrange("p (t d) -> p t d", t=TPQ),
                             x_in[q * UT:(q + 1) * UT, :].rearrange("(t p) d -> p t d", p=P)).then_inc(x_loaded[q], 16)
            for n in range(2, 2 * NC):
                sp.wait_ge(raw_split, n - 1)
                load_qkv(0, n) if n < NC else load_o(0, n - NC)
            with sp.Fori(1, NKV) as g:
                load_group(g, False)
            sp.wait_ge(added, 4 * (UNITS + 1))
            sp.dma_start(w_raw[:], w_ffn.rearrange("(t p) d -> p t d", p=P)).then_inc(ffn_loaded, 16)
            sp.dma_start(c_raw[:], cents).then_inc(ffn_loaded, 16)
            sp.dma_start(bias_bc[:], b_ffn.rearrange("(a n) -> a n", a=1).broadcast_to([P, HID])).then_inc(ffn_loaded, 16)
            sp.dma_start(assign_bc[:], assign.rearrange("(a n) -> a n", a=1).broadcast_to([CLUSTERS, HID])).then_inc(ffn_loaded, 16)
            for q in range(QUADS):
                sp.wait_ge(final, TPQ * (q + 1))
                sp.dma_start(out[q * UT:(q + 1) * UT, :].rearrange("(t p) d -> p t d", p=P),
                             acc[:, q * TPQ * HID:(q + 1) * TPQ * HID].rearrange("p (t d) -> p t d", t=TPQ)).then_inc(stored, 16)
            sp.wait_ge(stored, 16 * QUADS)

        @block.gpsimd
        def _(pool):
            pool.memset(ident[:], 0.0).then_inc(pool_step, 1)
            pool.iota(dist[:], [[-1, SEQ]], base=P, channel_multiplier=1,
                      allow_small_or_imprecise_dtypes=True).then_inc(pool_step, 1)
            pool.wait_ge(pool_step, 2)
            pool.affine_select(out=ident[:], in_=ident[:], compare_op=ALU.not_equal, fill=1.0, base=0,
                               pattern=[[-1, P]], channel_multiplier=1).then_inc(ident_ready, 1)
            pool.tensor_scalar(dist[:], dist[:], 1.0, None, ALU.max).then_inc(dist_sq, 1)

            def split(slot, width, hi, lo, count):
                pool.sem_inc(pool_marks, 1)
                pool.tensor_scalar(hi, raw[:, slot, 0:width], 1.0, 1.0, ALU.mult, ALU.mult).then_inc(pool_step, 1)
                pool.wait_ge(pool_step, count)
                return pool.tensor_tensor(lo, raw[:, slot, 0:width], hi.bitcast(F32), ALU.subtract)

            def split_qkv(g):
                for c in range(NC):
                    pool.wait_ge(raw_loaded[c % 2], g * 128 + 48 * (c // 2 + 1))
                    i = split(c % 2, QKV_W, wqkv_hi[:, c, :], wqkv_lo[:, c, :], g * (2 * NC) + SETUP + c + 1)
                    i.then_inc(raw_split, 1)
                pool.wait_ge(raw_split, g * (2 * NC) + NC)
                pool.sem_inc(wqkv_ready, 1)

            def split_o(g):
                for h in range(HPG):
                    pool.wait_ge(raw_loaded[h % 2], g * 128 + 96 + 16 * (h // 2 + 1))
                    i = split(h % 2, HID, wo_hi[:, h, :], wo_lo[:, h, :], g * (2 * NC) + SETUP + NC + h + 1)
                    i.then_inc(raw_split, 1)
                pool.wait_ge(raw_split, g * (2 * NC) + 2 * NC)
                pool.sem_inc(wo_ready, 1)

            SETUP = 2
            split_qkv(0)
            pool.wait_ge(dist_ready, 1)
            pool.affine_select(out=dist[:], in_=dist[:], compare_op=ALU.not_equal, fill=0.0, base=P,
                               pattern=[[-1, SEQ]], channel_multiplier=1).then_inc(dist_sq, 1)
            pool.wait_ge(dist_sq, 2)
            pool.affine_select(out=dist[:], in_=dist[:], compare_op=ALU.is_ge, fill=MASKED, base=P,
                               pattern=[[-1, SEQ]], channel_multiplier=1).then_inc(dist_sq, 1)
            pool.wait_ge(dist_sq, 3)
            for h in range(HPG):
                i = pool.tensor_scalar(bias[:, h, :], dist[:], ALIBI_BASE ** (h + 1), 1.0, ALU.mult, ALU.mult)
                i.then_inc(dist_sq, 1)
            pool.wait_ge(dist_sq, 3 + HPG)
            pool.sem_inc(bias_ready, 1)
            split_o(0)
            with pool.Fori(1, NKV) as g:
                pool.wait_ge(qkv_mm, g * (PROJ_OUTS * QUADS))
                split_qkv(g)
                pool.wait_ge(scores_biased, g * (SCORE_BANKS * QUADS))
                pool.sem_inc(pool_marks, 1)
                pool.tensor_scalar(bias[:], bias[:], ALIBI_BASE ** HPG, 1.0, ALU.mult, ALU.mult).then_inc(bias_ready, 1)
                pool.wait_ge(wo_mm, g * (4 * QUADS) + 4)
                split_o(g)
            pool.wait_ge(added, 4 * (UNITS + 1))
            pool.memset(ones[:], 1.0).then_inc(ffn_consts, 1)
            pool.iota(cluster_id[:], [[0, 1]], base=0, channel_multiplier=1,
                      allow_small_or_imprecise_dtypes=True).then_inc(ffn_consts, 1)

        @block.scalar
        def _(act):
            act.sem_inc(pT_hi_done, CHUNKS)
            act.sem_inc(oT_hi_done, QTILES)
            act.wait_ge(dist_sq, 1)
            act.activation(bias[:, 0, :], dist[:], ACT.Sqrt).then_inc(dist_sqrt, 1)

            with act.Fori(0, QUADS) as q:
                act.wait_ge(var_ready, q + 1)
                act.activation(rs[:, 1, :], rs[:, 0, :], ACT.Sqrt).then_inc(std_ready, 1)
                for j in range(TPQ):
                    act.wait_ge(xn_mm, q * TPQ + TPQ + j + 1)
                    act.activation(xnT_hi[:, :, bass.ds(q * UT + j * P, P)],
                                   ps[:, j, :].rearrange("p (c t) -> p c t", c=NC), ACT.Copy).then_inc(xnT_hi_done, 1)

            def proj_hi(u, i):
                act.wait_ge(qkv_mm, u * PROJ_OUTS + i + 1)
                src = ps[:, PJ[i % 2], :]
                if i == 0:
                    ins = act.activation(kT_hi[:], src, ACT.Copy)
                elif i == PROJ_OUTS - 1:
                    ins = act.activation(vT[:], src, ACT.Copy)
                else:
                    ins = act.activation(qT_hi[:, i - 1, :], src, ACT.Copy, scale=SCALE)
                ins.then_inc(qkv_hi_done, 1)

            def pT_hi_part(u, c):
                act.wait_ge(pT_mm, u * CHUNKS + c + 1)
                act.activation(pT_hi[:, c % 2, :], ps[:, TR[c % 2], :], ACT.Copy).then_inc(pT_hi_done, 1)

            def oT_hi_part(u, k):
                act.wait_ge(pv_mm, u * QTILES + k + 1)
                act.activation(oT_hi[:, k % 3, :], ps[:, PV[k % 2], :], ACT.Copy).then_inc(oT_hi_done, 1)

            def exps(u, i):
                b, qt, heads = score_slices(i)
                act.wait_ge(scores_biased, u * SCORE_BANKS + i + 1)
                first, _ = stat_cols(i)
                for n, (h, col, _, keys, _) in enumerate(heads):
                    s = prob[:, i, col:col + keys]
                    ins = act.activation(s, s, ACT.Exp, bias=negmax[:, first + n:first + n + 1], scale=-1.0,
                                         accum_out=rowsum[:, first + n:first + n + 1])
                ins.then_inc(exp_done, 1)

            def body(u, proj, attn):
                for i in range(PROJ_OUTS):
                    if proj:
                        proj_hi(u, i)
                    if attn:
                        pT_hi_part(u, i)
                        if i in (1, 3, 4):
                            oT_hi_part(u, {1: 0, 3: 1, 4: 2}[i])
                if attn:
                    oT_hi_part(u, 3)
                if proj:
                    exps(u, 0)
                    act.wait_ge(v_mm, u + 1)
                    act.activation(v_hi[:], ps[:, TR[0], :].rearrange("p (t d) -> p t d", t=TPQ), ACT.Copy).then_inc(v_hi_done, 1)
                    for i in range(1, SCORE_BANKS):
                        exps(u, i)

            body(0, True, False)
            with act.Fori(1, UNITS) as u:
                body(u, True, True)
            body(UNITS, False, True)

            for c in range(NC):
                act.wait_ge(wT_mm, c + 1)
                act.activation(wT_hi[:, c, :], ps[:, TR[0] + c, :], ACT.Copy).then_inc(wT_hi_done, 1)
            act.wait_ge(wT_mm, NC + 1)
            act.activation(cT_hi[:], ps[:, SC[1], 0:NC * CLUSTERS].rearrange("p (c n) -> p c n", c=NC), ACT.Copy).then_inc(wT_hi_done, 1)
            act.sem_inc(cl_exp_done, 1)
            with act.Fori(0, QUADS) as q:
                act.wait_ge(var_ready, q + QUADS + 1)
                act.activation(rs[:, 1, :], rs[:, 0, :], ACT.Sqrt).then_inc(std_ready, 1)
                for j in range(TPQ):
                    act.wait_ge(x2_mm, q * TPQ + TPQ + j + 1)
                    act.activation(x2T_hi[:, :, j * P:(j + 1) * P],
                                   ps[:, TR[0] + j, :].rearrange("p (c t) -> p c t", c=NC), ACT.Copy).then_inc(x2T_hi_done, 1)
                act.wait_ge(cl_max_done, q + 1)
                for j in range(TPQ):
                    ins = act.activation(cl_exp[:, j, :], ps[:, SC[0], j * CLUSTERS:(j + 1) * CLUSTERS], ACT.Exp,
                                         bias=cl_bias[:, j:j + 1], scale=INV_TEMP, accum_out=cl_sum[:, j:j + 1])
                ins.then_inc(cl_exp_done, 1)

        @block.vector
        def _(dve):
            steps = [0]

            def step(ins):
                steps[0] += 1
                ins.then_inc(dve_step, 1)
                dve.wait_ge(dve_step, steps[0])

            dve.sem_inc(pT_lo_done, CHUNKS)
            dve.sem_inc(oT_lo_done, QTILES)
            dve.sem_inc(added, QTILES)

            dve.wait_ge(dist_sqrt, 1)
            step(dve.reciprocal(bias[:, 1, :], bias[:, 0, :]))
            step(dve.tensor_tensor(bias[:, 2, :], bias[:, 1, :], dist[:], ALU.mult))
            step(dve.tensor_tensor(bias[:, 3, :], bias[:, 2, :], bias[:, 0, :], ALU.add))
            dve.tensor_scalar(dist[:], bias[:, 3, :], -0.5, None, ALU.mult).then_inc(dist_ready, 1)

            BASE1 = steps[0]
            PER_QUAD = 8
            for q in range(QUADS):
                n = [0]

                def chained(ins):
                    n[0] += 1
                    ins.then_inc(dve_step, 1)
                    dve.wait_ge(dve_step, q * PER_QUAD + BASE1 + n[0])

                dve.wait_ge(x_loaded[q], 16)
                for j in range(TPQ):
                    ins = dve.bn_stats(stats[:, j, :], acc[:, bass.ds(q * (TPQ * HID) + j * HID, HID)])
                chained(ins)
                dve.sem_inc(dve_marks, 1)
                for j in range(TPQ):
                    ins = dve.bn_aggr(meanvar[:, j, :], stats[:, j, :])
                chained(ins)
                dve.tensor_scalar(rs[:, 0, :], meanvar[:, :, 1], LN_EPS, None, ALU.add).then_inc(var_ready, 1)
                dve.wait_ge(std_ready, q + 1)
                chained(dve.reciprocal(rs[:, 2, :], rs[:, 1, :]))
                chained(dve.tensor_tensor(rs[:, 3, :], rs[:, 2, :], rs[:, 2, :], ALU.mult))
                chained(dve.tensor_tensor(rs[:, 4, :], rs[:, 3, :], rs[:, 0, :], ALU.mult))
                chained(dve.tensor_scalar(rs[:, 3, :], rs[:, 4, :], -0.5, 1.5, ALU.mult, ALU.add))
                chained(dve.tensor_tensor(rs[:, 5, :], rs[:, 3, :], rs[:, 2, :], ALU.mult))
                chained(dve.tensor_copy(rs[:, 4, :], meanvar[:, :, 0]))
                for j in range(TPQ):
                    dve.wait_ge(xn_mm, q * TPQ + j + 1)
                    dve.tensor_scalar(prob[:, j, :], acc[:, bass.ds(q * (TPQ * HID) + j * HID, HID)],
                                      rs[:, 4, j:j + 1], rs[:, 5, j:j + 1], ALU.subtract, ALU.mult).then_inc(xn_ready, 1)
                for j in range(TPQ):
                    dve.wait_ge(xnT_hi_done, q * TPQ + j + 1)
                    at = bass.ds(q * UT + j * P, P)
                    dve.tensor_tensor(xnT_lo[:, :, at], ps[:, j, :].rearrange("p (c t) -> p c t", c=NC),
                                      xnT_hi[:, :, at].bitcast(F32), ALU.subtract).then_inc(xnT_lo_done, 1)

            def proj_lo(u, i):
                dve.wait_ge(qkv_hi_done, u * PROJ_OUTS + i + 1)
                src = ps[:, PJ[i % 2], :]
                if i == 0:
                    ins = dve.tensor_tensor(kT_lo[:], src, kT_hi[:].bitcast(F32), ALU.subtract)
                else:
                    ins = dve.scalar_tensor_tensor(qT_lo[:, i - 1, :], src, SCALE, qT_hi[:, i - 1, :].bitcast(F32),
                                                   ALU.mult, ALU.subtract)
                ins.then_inc(qk_lo_done, 1)

            def pT_lo_part(u, c):
                dve.wait_ge(pT_hi_done, u * CHUNKS + c + 1)
                dve.tensor_tensor(pT_lo[:, c % 2, :], ps[:, TR[c % 2], :], pT_hi[:, c % 2, :].bitcast(F32),
                                  ALU.subtract).then_inc(pT_lo_done, 1)

            def oT_lo_part(u, k):
                dve.wait_ge(oT_hi_done, u * QTILES + k + 1)
                dve.tensor_tensor(oT_lo[:, k % 3, :], ps[:, PV[k % 2], :], oT_hi[:, k % 3, :].bitcast(F32),
                                  ALU.subtract).then_inc(oT_lo_done, 1)

            def add_out(u, k):
                dve.wait_ge(wo_mm, u * QTILES + k + 1)
                at = bass.ds(quad_of(u + QUADS - 1) * (TPQ * HID) + k * HID, HID)
                dve.tensor_tensor(acc[:, at], ps[:, PJ[k % 2], :], acc[:, at], ALU.add).then_inc(added, 1)

            def add_bias(u, i):
                b, qt, heads = score_slices(i)
                if i == 0:
                    dve.wait_ge(bias_ready, group_count(u))
                dve.wait_ge(s_mm, u * SCORE_BANKS + i + 1)
                dve.sem_inc(dve_marks, 1)
                first, _ = stat_cols(i)
                for n, (h, col, _, keys, _) in enumerate(heads):
                    ins = dve.tensor_tensor_reduce(
                        out=prob[:, i, col:col + keys], in0=ps[:, SC[i % 2], col:col + keys],
                        in1=bias[:, h, SEQ - keys:SEQ], scale=-1.0, scalar=BIGGEST, op0=ALU.add, op1=ALU.min,
                        accum_out=negmax[:, first + n:first + n + 1])
                ins.then_inc(scores_biased, 1)

            def normalise(u, i):
                b, qt, heads = score_slices(i)
                first, end = stat_cols(i)
                dve.wait_ge(exp_done, u * SCORE_BANKS + i + 1)
                dve.reciprocal(rinv[:, first:end], rowsum[:, first:end]).then_inc(rinv_done, 1)
                dve.wait_ge(rinv_done, u * SCORE_BANKS + i + 1)
                for n, (h, col, _, keys, _) in enumerate(heads):
                    s = prob[:, i, col:col + keys]
                    ins = dve.tensor_scalar(s, s, rinv[:, first + n:first + n + 1], None, ALU.mult)
                ins.then_inc(probs_ready, 1)

            def body(u, proj, attn):
                for i in range(PROJ_OUTS):
                    if proj and i < PROJ_OUTS - 1:
                        proj_lo(u, i)
                    if attn:
                        pT_lo_part(u, i)
                        if i in (1, 3, 4):
                            oT_lo_part(u, {1: 0, 3: 1, 4: 2}[i])
                if attn:
                    oT_lo_part(u, 3)
                    add_out(u, 0)
                if proj:
                    add_bias(u, 0)
                    dve.wait_ge(v_hi_done, u + 1)
                    dve.tensor_tensor(v_lo[:], ps[:, TR[0], :].rearrange("p (t d) -> p t d", t=TPQ),
                                      v_hi[:].bitcast(F32), ALU.subtract).then_inc(v_lo_done, 1)
                    normalise(u, 0)
                if attn:
                    add_out(u, 1)
                if proj:
                    add_bias(u, 1)
                    add_bias(u, 2)
                    normalise(u, 1)
                if attn:
                    add_out(u, 2)
                if proj:
                    add_bias(u, 3)
                    normalise(u, 2)
                    add_bias(u, 4)
                    normalise(u, 3)
                if attn:
                    add_out(u, 3)
                if proj:
                    add_bias(u, 5)
                    normalise(u, 4)
                    normalise(u, 5)

            body(0, True, False)
            with dve.Fori(1, UNITS) as u:
                body(u, True, True)
            body(UNITS, False, True)

            dve.wait_ge(added, 4 * (UNITS + 1))
            for c in range(NC):
                dve.wait_ge(wT_hi_done, c + 1)
                dve.tensor_tensor(wT_lo[:, c, :], ps[:, TR[0] + c, :], wT_hi[:, c, :].bitcast(F32),
                                  ALU.subtract).then_inc(wT_lo_done, 1)
            dve.wait_ge(wT_hi_done, NC + 1)
            dve.tensor_tensor(cT_lo[:], ps[:, SC[1], 0:NC * CLUSTERS].rearrange("p (c n) -> p c n", c=NC),
                              cT_hi[:].bitcast(F32), ALU.subtract).then_inc(wT_lo_done, 1)
            dve.wait_ge(ffn_loaded, 64)
            dve.wait_ge(ffn_consts, 2)
            base2 = BASE1 + QUADS * PER_QUAD
            dve.tensor_copy(assign_f[:], assign_bc[:]).then_inc(dve_step, 1)
            dve.wait_ge(dve_step, base2 + 1)
            dve.tensor_scalar(onehot[:], assign_f[:], cluster_id[:], None, ALU.is_equal).then_inc(dve_step, 1)
            BASE2 = base2 + 2
            dve.sem_inc(dense_out, TPQ)
            PER_FFN = PER_QUAD + 4 + TPQ
            with dve.Fori(0, QUADS) as q:
                n = [0]

                def chained(ins):
                    n[0] += 1
                    ins.then_inc(dve_step, 1)
                    dve.wait_ge(dve_step, q * PER_FFN + BASE2 + n[0])

                for j in range(TPQ):
                    ins = dve.bn_stats(stats[:, j, :], acc[:, bass.ds(q * (TPQ * HID) + j * HID, HID)])
                chained(ins)
                dve.sem_inc(dve_marks, 1)
                for j in range(TPQ):
                    ins = dve.bn_aggr(meanvar[:, j, :], stats[:, j, :])
                chained(ins)
                dve.tensor_scalar(rs[:, 0, :], meanvar[:, :, 1], LN_EPS, None, ALU.add).then_inc(var_ready, 1)
                dve.wait_ge(std_ready, q + QUADS + 1)
                chained(dve.reciprocal(rs[:, 2, :], rs[:, 1, :]))
                chained(dve.tensor_tensor(rs[:, 3, :], rs[:, 2, :], rs[:, 2, :], ALU.mult))
                chained(dve.tensor_tensor(rs[:, 4, :], rs[:, 3, :], rs[:, 0, :], ALU.mult))
                chained(dve.tensor_scalar(rs[:, 3, :], rs[:, 4, :], -0.5, 1.5, ALU.mult, ALU.add))
                chained(dve.tensor_tensor(rs[:, 5, :], rs[:, 3, :], rs[:, 2, :], ALU.mult))
                chained(dve.tensor_copy(rs[:, 4, :], meanvar[:, :, 0]))
                for j in range(TPQ):
                    dve.wait_ge(x2_mm, q * TPQ + j + 1)
                    dve.tensor_scalar(stage[:, j, :], acc[:, bass.ds(q * (TPQ * HID) + j * HID, HID)],
                                      rs[:, 4, j:j + 1], rs[:, 5, j:j + 1], ALU.subtract, ALU.mult).then_inc(x2_ready, 1)
                for j in range(TPQ):
                    dve.wait_ge(x2T_hi_done, q * TPQ + j + 1)
                    dve.tensor_tensor(x2T_lo[:, :, j * P:(j + 1) * P], ps[:, TR[0] + j, :].rearrange("p (c t) -> p c t", c=NC),
                                      x2T_hi[:, :, j * P:(j + 1) * P].bitcast(F32), ALU.subtract).then_inc(x2T_lo_done, 1)
                dve.wait_ge(logit_mm, q + 1)
                logits = ps[:, SC[0], 0:TPQ * CLUSTERS].rearrange("p (t c) -> p t c", t=TPQ)
                chained(dve.tensor_reduce(cl_nmax[:], logits, AX_X, ALU.max, negate=True))
                dve.tensor_scalar(cl_bias[:], cl_nmax[:], INV_TEMP, None, ALU.mult).then_inc(cl_max_done, 1)
                dve.wait_ge(cl_exp_done, q + 2)
                chained(dve.reciprocal(cl_rinv[:], cl_sum[:]))
                for j in range(TPQ):
                    ins = dve.tensor_scalar(hits[:, bass.ds(q * (TPQ * CLUSTERS) + j * CLUSTERS, CLUSTERS)], cl_exp[:, j, :],
                                            cl_rinv[:, j:j + 1], THRESHOLD, ALU.mult, ALU.is_gt)
                chained(ins)
                dve.sem_inc(dve_marks, 1)
                chained(dve.tensor_reduce(query_sel[:], hits[:, bass.ds(q * (TPQ * CLUSTERS), TPQ * CLUSTERS)].rearrange(
                    "p (t c) -> p t c", t=TPQ), AX_X, ALU.max))
                for j in range(TPQ):
                    at = bass.ds(q * (TPQ * HID) + j * HID, HID)
                    dve.wait_ge(dense_mm, q * TPQ + j + 1)
                    ins = dve.tensor_tensor(fbias[:, j % 2, :], ps[:, PJ[j % 2], :], bias_bc[:], ALU.add)
                    chained(ins)
                    dve.scalar_tensor_tensor(selected[:, at], fbias[:, j % 2, :], query_sel[:, j:j + 1], acc[:, at],
                                             ALU.mult, ALU.add).then_inc(dense_out, 1)
                assert n[0] == PER_FFN, n
            dve.wait_ge(dense_out, TPQ * (QUADS + 1))
            dve.tensor_reduce(any_hit[:], hits[:].rearrange("p (t c) -> p c t", c=CLUSTERS), AX_X, ALU.max).then_inc(any_ready, 1)
            dve.wait_ge(sel_mm, 1)
            dve.tensor_scalar(cluster_sel[:], ps[0:CLUSTERS, TR[0], 0:P], 0.0, None, ALU.is_gt).then_inc(csel_ready, 1)
            dve.wait_ge(sel_mm, 2)
            for t in range(TILES):
                dve.copy_predicated(acc[:, t * HID:(t + 1) * HID], ps[:, TR[1], :].bitcast(I32),
                                    selected[:, t * HID:(t + 1) * HID]).then_inc(final, 1)

        @block.tensor
        def _(pe):
            def three_pass(dst, terms, start, stop):
                n = 3 * len(terms)
                m = 0
                for (l_hi, l_lo), (r_hi, r_lo) in terms:
                    for l, r in ((l_hi, r_hi), (l_hi, r_lo), (l_lo, r_hi)):
                        ins = pe.matmul(dst, l, r, start=start and m == 0, stop=stop and m == n - 1)
                        m += 1
                return ins

            pe.sem_inc(xn_mm, TPQ)
            pe.sem_inc(x2_mm, TPQ)
            pe.sem_inc(pT_mm, CHUNKS)
            pe.sem_inc(pv_mm, QTILES)
            pe.sem_inc(wo_mm, QTILES)
            pe.wait_ge(ident_ready, 1)
            with pe.Fori(0, QUADS) as q:
                for j in range(TPQ):
                    pe.wait_ge(xn_ready, q * TPQ + j + 1)
                    for c in range(NC):
                        ins = pe.transpose(ps[:, j, c * P:(c + 1) * P], prob[:, j, c * P:(c + 1) * P], ident[:])
                    ins.then_inc(xn_mm, 1)
            pe.wait_ge(xnT_lo_done, TILES)

            def project(u, i):
                if i == 0:
                    pe.wait_ge(wqkv_ready, group_count(u))
                col = HPG * D if i == 0 else (HPG + 1) * D if i == PROJ_OUTS - 1 else (i - 1) * D
                at = bass.ds(quad_of(u) * UT, UT)
                terms = [((wqkv_hi[:, c, col:col + D], wqkv_lo[:, c, col:col + D]),
                          (xnT_hi[:, c, at], xnT_lo[:, c, at])) for c in range(NC)]
                three_pass(ps[:, PJ[i % 2], :], terms, True, True).then_inc(qkv_mm, 1)

            def transpose_probs(u, c):
                b, qt, kt, blocks = chunk_blocks(c)
                pe.wait_ge(probs_ready, u * SCORE_BANKS - SCORE_BANKS + 3 * b + (1 if qt == 0 else 3))
                for h, (bank, col) in enumerate(blocks):
                    ins = pe.transpose(ps[:, TR[c % 2], h * P:(h + 1) * P], prob[:, bank, col:col + P], ident[:])
                ins.then_inc(pT_mm, 1)

            def apply_v(u, c):
                b, qt, kt, _ = chunk_blocks(c)
                k = 2 * b + qt
                pe.wait_ge(pT_lo_done, u * CHUNKS + c + 1)
                if kt == 0:
                    pe.wait_ge(oT_lo_done, u * QTILES + k - 1)
                t = 2 * b + kt
                ins = three_pass(ps[:, PV[k % 2], :], [((v_hi[:, t, :], v_lo[:, t, :]), (pT_hi[:, c % 2, :], pT_lo[:, c % 2, :]))],
                                 kt == 0, kt == qt)
                if kt == qt:
                    ins.then_inc(pv_mm, 1)

            def project_out(u, k):
                pe.wait_ge(oT_lo_done, u * QTILES + k + 1)
                terms = [((oT_hi[:, k % 3, h * P:(h + 1) * P], oT_lo[:, k % 3, h * P:(h + 1) * P]),
                          (wo_hi[:, h, :], wo_lo[:, h, :])) for h in range(HPG)]
                three_pass(ps[:, PJ[k % 2], :], terms, True, True).then_inc(wo_mm, 1)

            def scores(u, i):
                b, qt, heads = score_slices(i)
                if not (isinstance(u, int) and i < 2):
                    pe.wait_ge(scores_biased, u * SCORE_BANKS + i - 1)
                for h, col, _, keys, _ in heads:
                    q0 = b * SEQ + qt * P
                    q_at, k_at = slice(q0, q0 + P), slice(b * SEQ, b * SEQ + keys)
                    ins = three_pass(ps[:, SC[i % 2], col:col + keys],
                                     [((qT_hi[:, h, q_at], qT_lo[:, h, q_at]), (kT_hi[:, k_at], kT_lo[:, k_at]))], True, True)
                ins.then_inc(s_mm, 1)

            def body(u, proj, attn):
                for i in range(PROJ_OUTS):
                    if proj:
                        if i < 2:
                            if attn:
                                pe.wait_ge(added, u * QTILES + i - 1)
                        else:
                            pe.wait_ge(qk_lo_done, u * 5 + i - 1)
                        project(u, i)
                    if attn:
                        if i == 0:
                            pe.wait_ge(v_lo_done, u)
                        else:
                            pe.wait_ge(pT_lo_done, u * CHUNKS + i - 1)
                        transpose_probs(u, i)
                        if i > 0:
                            apply_v(u, i - 1)
                if attn:
                    if proj:
                        pe.wait_ge(qk_lo_done, u * 5 + 5)
                    else:
                        pe.wait_ge(added, u * QTILES - 1)
                    pe.wait_ge(wo_ready, group_count(u - 1))
                    project_out(u, 0)
                    apply_v(u, CHUNKS - 1)
                if proj:
                    if not attn:
                        pe.wait_ge(qk_lo_done, 5)
                    scores(u, 0)
                    pe.wait_ge(qkv_hi_done, u * PROJ_OUTS + 6)
                    pe.wait_ge(pT_lo_done, u * CHUNKS + 5)
                    for t in range(TPQ):
                        ins = pe.transpose(ps[:, TR[0], t * P:(t + 1) * P], vT[:, t * P:(t + 1) * P], ident[:])
                    ins.then_inc(v_mm, 1)
                if attn:
                    if not proj:
                        pe.wait_ge(added, u * QTILES)
                    project_out(u, 1)
                if proj:
                    scores(u, 1)
                    scores(u, 2)
                if attn:
                    pe.wait_ge(added, u * QTILES + 1)
                    project_out(u, 2)
                if proj:
                    scores(u, 3)
                    scores(u, 4)
                if attn:
                    pe.wait_ge(added, u * QTILES + 2)
                    project_out(u, 3)
                if proj:
                    scores(u, 5)

            body(0, True, False)
            with pe.Fori(1, UNITS) as u:
                body(u, True, True)
            body(UNITS, False, True)

            pe.wait_ge(added, 4 * (UNITS + 1))
            pe.wait_ge(ffn_loaded, 64)
            for c in range(NC):
                for t in range(NC):
                    ins = pe.transpose(ps[:, TR[0] + c, t * P:(t + 1) * P], w_raw[:, t, c * P:(c + 1) * P], ident[:])
                ins.then_inc(wT_mm, 1)
            for c in range(NC):
                ins = pe.transpose(ps[:, SC[1], c * CLUSTERS:(c + 1) * CLUSTERS], c_raw[:, c * P:(c + 1) * P],
                                   ident[0:CLUSTERS, 0:CLUSTERS])
            ins.then_inc(wT_mm, 1)
            pe.wait_ge(wT_lo_done, NC + 1)
            with pe.Fori(0, QUADS) as q:
                for j in range(TPQ):
                    pe.wait_ge(x2_ready, q * TPQ + j + 1)
                    for c in range(NC):
                        ins = pe.transpose(ps[:, TR[0] + j, c * P:(c + 1) * P], stage[:, j, c * P:(c + 1) * P], ident[:])
                    ins.then_inc(x2_mm, 1)
                pe.wait_ge(x2T_lo_done, q * TPQ + TPQ)
                pe.wait_ge(cl_exp_done, q + 1)
                for j in range(TPQ):
                    at = slice(j * P, (j + 1) * P)
                    terms = [((x2T_hi[:, c, at], x2T_lo[:, c, at]), (cT_hi[:, c, :], cT_lo[:, c, :])) for c in range(NC)]
                    ins = three_pass(ps[:, SC[0], j * CLUSTERS:(j + 1) * CLUSTERS], terms, True, True)
                ins.then_inc(logit_mm, 1)
                for j in range(TPQ):
                    at = slice(j * P, (j + 1) * P)
                    pe.wait_ge(dense_out, q * TPQ + j + 3)
                    terms = [((x2T_hi[:, c, at], x2T_lo[:, c, at]), (wT_hi[:, c, :], wT_lo[:, c, :])) for c in range(NC)]
                    three_pass(ps[:, PJ[j % 2], :], terms, True, True).then_inc(dense_mm, 1)
            pe.wait_ge(any_ready, 1)
            pe.matmul(ps[0:CLUSTERS, TR[0], 0:P], any_hit[:], ones[:], start=True, stop=True).then_inc(sel_mm, 1)
            pe.wait_ge(csel_ready, 1)
            pe.matmul(ps[:, TR[1], :], cluster_sel[:], onehot[:], start=True, stop=True).then_inc(sel_mm, 1)


_INS = ['L0_attn_hidden_states', 'L0_attn_w_qkv', 'L0_attn_w_o', 'L0_ffn_weight', 'L0_ffn_bias', 'L0_ffn_centroids',
        'L0_ffn_assignments']


def kernel(**inputs):
    import numpy as np
    import concourse.bacc as bacc
    from concourse.bass_utils import run_bass_kernel_spmd

    nc = bacc.Bacc("TRN2", target_bir_lowering=False, num_devices=1)
    arrays, args = {}, []
    for name in _INS:
        a = np.ascontiguousarray(inputs[name])
        if name == 'L0_attn_hidden_states':
            a = a.reshape(TOK, HID)
        arrays[f"in_{name}"] = a
        args.append(nc.dram_tensor(f"in_{name}", a.shape, mybir.dt.from_np(a.dtype), kind="ExternalInput").ap())
    args.append(nc.dram_tensor("out", [TOK, HID], F32, kind="ExternalOutput").ap())
    build(nc, *args)
    r = run_bass_kernel_spmd(nc, [arrays], core_ids=[0])
    return r.results[0]["out"].reshape(BATCH, SEQ, HID)
```

```python
from contextlib import ExitStack

import concourse.bass as bass
from concourse import mybir

ALU = mybir.AluOpType
ACT = mybir.ActivationFunctionType
F32 = mybir.dt.float32
F32R = mybir.dt.float32r
BF16 = mybir.dt.bfloat16
I32 = mybir.dt.int32
AX_X = mybir.AxisListType.X

P = 128
BATCH, SEQ, HID = 8, 256, 512
NH, NKV, D = 32, 8, 128
HPG = NH // NKV
TOK = BATCH * SEQ
TILES = TOK // P
NC = HID // P
UT = 512
QUADS = TOK // UT
TPQ = UT // P
UNITS = NKV * QUADS
QKV_W = (HPG + 2) * D
SCALE = float(D) ** -0.5
LN_EPS = 1e-5
MASKED = -3.0e38
BIGGEST = 3.0e38
CLUSTERS = 64
INV_TEMP = 1.0 / 0.10000000149011612
THRESHOLD = 0.01
ALIBI_BASE = 2.0 ** (-8.0 / NH)

PROJ_OUTS = 6
CHUNKS = 6
SCORE_BANKS = 8
PROB_TILES = 6
QTILES = 4


def build(nc, x_in, w_qkv, w_o, w_ffn, b_ffn, cents, assign, out):
    ctx = ExitStack()
    with ctx:
        def sem(name):
            return ctx.enter_context(nc.semaphore(name))

        def sb(name, shape, dt, where=ctx):
            return where.enter_context(nc.sbuf_tensor(name, shape, dt))

        acc = sb("acc", [P, TILES * HID], F32)
        ident = sb("ident", [P, P], F32)
        stats = sb("stats", [P, TPQ, 6], F32)
        meanvar = sb("meanvar", [P, TPQ, 2], F32)
        rs = sb("rs", [P, 6, TPQ], F32)
        onehot = sb("onehot", [CLUSTERS, HID], BF16)
        ones = sb("ones", [P, P], BF16)
        cluster_id = sb("cluster_id", [CLUSTERS, 1], F32)
        cl_nmax = sb("cl_nmax", [P, TPQ], F32)
        cl_bias = sb("cl_bias", [P, TPQ], F32)
        cl_sum = sb("cl_sum", [P, TPQ], F32)
        cl_rinv = sb("cl_rinv", [P, TPQ], F32)
        query_sel = sb("query_sel", [P, TPQ], F32)

        att = ExitStack()
        xnT = sb("xnT", [P, QUADS, 2, NC, UT], F32R, att)
        raw = sb("raw", [P, 2, QKV_W], F32, att)
        wqkv_hi = sb("wqkv_hi", [P, NC, QKV_W], F32R, att)
        wqkv_lo = sb("wqkv_lo", [P, NC, QKV_W], F32R, att)
        wo_hi = sb("wo_hi", [P, HPG, HID], F32R, att)
        wo_lo = sb("wo_lo", [P, HPG, HID], F32R, att)
        qT_hi = sb("qT_hi", [P, HPG, UT], F32R, att)
        qT_lo = sb("qT_lo", [P, HPG, UT], F32R, att)
        kT = sb("kT", [P, TPQ, 2, P], F32R, att)
        vT = sb("vT", [P, UT], F32, att)
        v_hi = sb("v_hi", [P, TPQ, D], F32R, att)
        v_lo = sb("v_lo", [P, TPQ, D], F32R, att)
        prob = sb("prob", [P, PROB_TILES, 512], F32, att)
        pT_hi = sb("pT_hi", [P, 2, 512], F32R, att)
        pT_lo = sb("pT_lo", [P, 2, 512], F32R, att)
        oT_hi = sb("oT_hi", [P, 3, 512], F32R, att)
        oT_lo = sb("oT_lo", [P, 3, 512], F32R, att)
        bias = sb("bias", [P, HPG, SEQ], F32, att)
        dist = sb("dist", [P, SEQ], F32, att)
        negmax = sb("negmax", [P, 16], F32, att)
        rowsum = sb("rowsum", [P, 16], F32, att)
        rinv = sb("rinv", [P, 16], F32, att)
        att.close()

        x2T_hi, x2T_lo = xnT[:, 0, 0], xnT[:, 0, 1]
        wT_hi, wT_lo = xnT[:, 1, 0], xnT[:, 1, 1]
        cl_exp = dist
        ffn = ExitStack()
        w_raw = sb("w_raw", [P, NC, HID], F32, ffn)
        c_raw = sb("c_raw", [CLUSTERS, HID], F32, ffn)
        sb("gap", [P, 22 * 256], F32, ffn)
        selected = sb("selected", [P, TILES * HID], F32, ffn)
        cT_hi = sb("cT_hi", [P, NC, CLUSTERS], F32R, ffn)
        cT_lo = sb("cT_lo", [P, NC, CLUSTERS], F32R, ffn)
        bias_bc = sb("bias_bc", [P, HID], F32, ffn)
        quad_hits = sb("quad_hits", [P, QUADS * CLUSTERS], BF16, ffn)
        any_hit = sb("any_hit", [P, CLUSTERS], BF16, ffn)
        cluster_sel = sb("cluster_sel", [CLUSTERS, P], BF16, ffn)
        ffn.close()

        ps = ctx.enter_context(nc.psum_tensor("ps", [P, 8, 512], F32))
        PJ = (0, 1)
        TR = (2, 3)
        PV = (4, 5)
        SC = (6, 7)

        x_loaded = [sem(f"x_loaded{q}") for q in range(QUADS)]
        raw_loaded = [sem("raw_loaded0"), sem("raw_loaded1")]
        assign_loaded = sem("assign_loaded")
        wc_loaded = sem("wc_loaded")
        bias_loaded = sem("bias_loaded")
        stored = sem("stored")
        pool_step = sem("pool_step")
        pool_marks = sem("pool_marks")
        ident_ready = sem("ident_ready")
        dist_sq = sem("dist_sq")
        raw_split = sem("raw_split")
        wqkv_ready = sem("wqkv_ready")
        wo_ready = sem("wo_ready")
        bias_ready = sem("bias_ready")
        ffn_consts = sem("ffn_consts")
        ln_mm = sem("ln_mm")
        qkv_mm = sem("qkv_mm")
        pT_mm = sem("pT_mm")
        pv_mm = sem("pv_mm")
        wo_mm = sem("wo_mm")
        s_mm = sem("s_mm")
        v_mm = sem("v_mm")
        wT_mm = sem("wT_mm")
        logit_mm = sem("logit_mm")
        dense_mm = sem("dense_mm")
        sel_mm = sem("sel_mm")
        w_hi_done = sem("w_hi_done")
        dist_sqrt = sem("dist_sqrt")
        std_ready = sem("std_ready")
        ln_hi_done = sem("ln_hi_done")
        qkv_hi_done = sem("qkv_hi_done")
        pT_hi_done = sem("pT_hi_done")
        oT_hi_done = sem("oT_hi_done")
        exp_done = sem("exp_done")
        v_hi_done = sem("v_hi_done")
        wT_hi_done = sem("wT_hi_done")
        cl_exp_done = sem("cl_exp_done")
        dve_step = sem("dve_step")
        dist_ready = sem("dist_ready")
        var_ready = sem("var_ready")
        ln_step = sem("ln_step")
        ln_ready = sem("ln_ready")
        ln_lo_done = sem("ln_lo_done")
        ffn_step = sem("ffn_step")
        onehot_ready = sem("onehot_ready")
        qk_lo_done = sem("qk_lo_done")
        pT_lo_done = sem("pT_lo_done")
        oT_lo_done = sem("oT_lo_done")
        scores_biased = sem("scores_biased")
        lo_biased = sem("lo_biased")
        dve_marks = sem("dve_marks")
        rinv_done = sem("rinv_done")
        probs_ready = sem("probs_ready")
        v_lo_done = sem("v_lo_done")
        added = sem("added")
        wT_lo_done = sem("wT_lo_done")
        cl_max_done = sem("cl_max_done")
        hits_done = sem("hits_done")
        dense_out = sem("dense_out")
        any_ready = sem("any_ready")
        csel_ready = sem("csel_ready")
        final = sem("final")

        block = ctx.enter_context(nc.Block())

        WT_BANKS = (SC[0], SC[1], PV[0], PV[1], TR[1])

        def group_count(u):
            return (u + QUADS) >> 2

        def quad_of(u):
            return u % QUADS

        def rows(q, j=0, n=TPQ):
            return bass.ds(q * (TPQ * HID) + j * HID, n * HID)

        def ln_part(quad, part, j):
            if isinstance(quad, int):
                return xnT[:, quad, part, :, j * P:(j + 1) * P]
            flat = xnT[:].rearrange("p q s c t -> p (q s c t)")
            at = quad * (2 * NC * UT) + part * (NC * UT)
            return flat[:, bass.ds(at, NC * UT)].rearrange("p (c t) -> p c t", c=NC)[:, :, j * P:(j + 1) * P]

        LN_AFTER_CHUNK = (0, 2, 2, 3)

        def score_slices(i):
            b, qt, pair = i // 4, i // 2 % 2, i % 2
            heads = (2 * pair, 2 * pair + 1)
            if qt == 0:
                return b, qt, [(h, (h % 2) * SEQ, 3 * b, h * P, 8 * b + h) for h in heads]
            return b, qt, [(h, (h % 2) * SEQ, 3 * b + 1 + pair, (h % 2) * SEQ, 8 * b + HPG + h) for h in heads]

        def chunk_blocks(c):
            b, part = c // 3, c % 3
            if part == 0:
                return b, 0, 0, [(3 * b, h * P) for h in range(HPG)]
            kt = part - 1
            return b, 1, kt, [(3 * b + 1 + h // 2, (h % 2) * SEQ + kt * P) for h in range(HPG)]

        @block.sync
        def _(sp):
            def load_qkv(g, c):
                rows = w_qkv[c * P:(c + 1) * P, :]
                slot = raw[:, c % 2, :]
                done = raw_loaded[c % 2]
                sp.dma_start(slot[:, 0:HPG * D], rows[:, bass.ds(g * (HPG * D), HPG * D)]).then_inc(done, 16)
                sp.dma_start(slot[:, HPG * D:HPG * D + D], rows[:, bass.ds(g * D + NH * D, D)]).then_inc(done, 16)
                sp.dma_start(slot[:, HPG * D + D:QKV_W], rows[:, bass.ds(g * D + (NH + NKV) * D, D)]).then_inc(done, 16)

            def load_o(g, h):
                rows = w_o[bass.ds(g * (HPG * D) + h * D, D), :]
                sp.dma_start(raw[:, h % 2, 0:HID], rows).then_inc(raw_loaded[h % 2], 16)

            def load_group(g, first):
                for n in range(2 * NC):
                    if not (first and n < 2):
                        sp.wait_ge(raw_split, g * (2 * NC) + n - 1)
                    load_qkv(g, n) if n < NC else load_o(g, n - NC)

            load_qkv(0, 0)
            sp.dma_start(acc[:, 0:TPQ * HID].rearrange("p (t d) -> p t d", t=TPQ),
                         x_in[0:UT, :].rearrange("(t p) d -> p t d", p=P)).then_inc(x_loaded[0], 16)
            load_qkv(0, 1)
            for n in range(2, 2 * NC):
                if n == NC:
                    sp.dma_start(prob[0:CLUSTERS, 4, :].bitcast(I32),
                                 assign.rearrange("(a n) -> a n", a=1).broadcast_to([CLUSTERS, HID])).then_inc(assign_loaded, 16)
                    for q in range(1, QUADS):
                        sp.dma_start(acc[:, q * TPQ * HID:(q + 1) * TPQ * HID].rearrange("p (t d) -> p t d", t=TPQ),
                                     x_in[q * UT:(q + 1) * UT, :].rearrange("(t p) d -> p t d", p=P)).then_inc(x_loaded[q], 16)
                sp.wait_ge(raw_split, n - 1)
                load_qkv(0, n) if n < NC else load_o(0, n - NC)
            with sp.Fori(1, NKV) as g:
                load_group(g, False)
            sp.wait_ge(qkv_mm, PROJ_OUTS * (UNITS - QUADS + 1))
            sp.dma_start(w_raw[:], w_ffn.rearrange("(t p) d -> p t d", p=P)).then_inc(wc_loaded, 16)
            sp.dma_start(c_raw[:], cents).then_inc(wc_loaded, 16)
            sp.wait_ge(raw_split, 2 * NC * NKV)
            sp.dma_start(bias_bc[:], b_ffn.rearrange("(a n) -> a n", a=1).broadcast_to([P, HID])).then_inc(bias_loaded, 16)
            for q in range(QUADS):
                sp.wait_ge(final, TPQ * (q + 1))
                sp.dma_start(out[q * UT:(q + 1) * UT, :].rearrange("(t p) d -> p t d", p=P),
                             acc[:, q * TPQ * HID:(q + 1) * TPQ * HID].rearrange("p (t d) -> p t d", t=TPQ)).then_inc(stored, 16)
            sp.wait_ge(stored, 16 * QUADS)

        @block.gpsimd
        def _(pool):
            pool.memset(ident[:], 0.0).then_inc(pool_step, 1)
            pool.memset(ones[:], 1.0).then_inc(ffn_consts, 1)
            pool.iota(cluster_id[:], [[0, 1]], base=0, channel_multiplier=1,
                      allow_small_or_imprecise_dtypes=True).then_inc(ffn_consts, 1)
            pool.iota(dist[:], [[-1, SEQ]], base=P, channel_multiplier=1,
                      allow_small_or_imprecise_dtypes=True).then_inc(pool_step, 1)
            pool.wait_ge(pool_step, 2)
            pool.affine_select(out=ident[:], in_=ident[:], compare_op=ALU.not_equal, fill=1.0, base=0,
                               pattern=[[-1, P]], channel_multiplier=1).then_inc(ident_ready, 1)
            pool.tensor_scalar(dist[:], dist[:], 1.0, None, ALU.max).then_inc(dist_sq, 1)

            def split(slot, width, hi, lo, count, first):
                pool.sem_inc(pool_marks, 1)
                if not first:
                    pool.tensor_scalar(hi, raw[:, slot, 0:width], 1.0, 1.0, ALU.mult, ALU.mult).then_inc(pool_step, 1)
                    pool.wait_ge(pool_step, count)
                return pool.tensor_tensor(lo, raw[:, slot, 0:width], hi.bitcast(F32), ALU.subtract)

            def split_qkv(g):
                for c in range(NC):
                    pool.wait_ge(raw_loaded[c % 2], g * 128 + 48 * (c // 2 + 1))
                    first = isinstance(g, int)
                    if first:
                        pool.wait_ge(w_hi_done, c + 1)
                    i = split(c % 2, QKV_W, wqkv_hi[:, c, :], wqkv_lo[:, c, :], g * (2 * NC) + SETUP + c + 1, first)
                    i.then_inc(raw_split, 1)
                pool.wait_ge(raw_split, g * (2 * NC) + NC)
                pool.sem_inc(wqkv_ready, 1)

            def split_o(g):
                for h in range(HPG):
                    pool.wait_ge(raw_loaded[h % 2], g * 128 + 96 + 16 * (h // 2 + 1))
                    i = split(h % 2, HID, wo_hi[:, h, :], wo_lo[:, h, :], g * (2 * NC) + SETUP + NC + h + 1, False)
                    i.then_inc(raw_split, 1)
                pool.wait_ge(raw_split, g * (2 * NC) + 2 * NC)
                pool.sem_inc(wo_ready, 1)

            SETUP = 2 - NC
            split_qkv(0)
            pool.wait_ge(dist_ready, 1)
            pool.affine_select(out=dist[:], in_=dist[:], compare_op=ALU.not_equal, fill=0.0, base=P,
                               pattern=[[-1, SEQ]], channel_multiplier=1).then_inc(dist_sq, 1)
            pool.wait_ge(dist_sq, 2)
            pool.affine_select(out=dist[:], in_=dist[:], compare_op=ALU.is_ge, fill=MASKED, base=P,
                               pattern=[[-1, SEQ]], channel_multiplier=1).then_inc(dist_sq, 1)
            pool.wait_ge(dist_sq, 3)
            for h in range(HPG):
                i = pool.tensor_scalar(bias[:, h, :], dist[:], ALIBI_BASE ** (h + 1), 1.0, ALU.mult, ALU.mult)
                i.then_inc(dist_sq, 1)
            pool.wait_ge(dist_sq, 3 + HPG)
            pool.sem_inc(bias_ready, 1)
            split_o(0)
            with pool.Fori(1, NKV) as g:
                pool.wait_ge(qkv_mm, g * (PROJ_OUTS * QUADS))
                split_qkv(g)
                pool.wait_ge(scores_biased, g * (SCORE_BANKS * QUADS))
                pool.sem_inc(pool_marks, 1)
                pool.tensor_scalar(bias[:], bias[:], ALIBI_BASE ** HPG, 1.0, ALU.mult, ALU.mult).then_inc(bias_ready, 1)
                pool.wait_ge(wo_mm, g * (4 * QUADS) + 4)
                split_o(g)

        @block.scalar
        def _(act):
            act.sem_inc(pT_hi_done, CHUNKS)
            act.sem_inc(oT_hi_done, QTILES)
            act.sem_inc(cl_exp_done, 1)
            def ln_root(L):
                act.wait_ge(var_ready, L + 1)
                act.activation(rs[:, 1, :], rs[:, 0, :], ACT.Sqrt).then_inc(std_ready, 1)

            def ln_hi(L, j, quad):
                act.wait_ge(ln_mm, L * TPQ + j + 1)
                act.activation(ln_part(quad, 0, j), ps[:, SC[j % 2], :].rearrange("p (c t) -> p c t", c=NC),
                               ACT.Copy).then_inc(ln_hi_done, 1)

            def proj_hi(u, i):
                act.wait_ge(qkv_mm, u * PROJ_OUTS + i + 1)
                src = ps[:, PJ[i % 2], :]
                if i == 0:
                    ins = act.activation(kT[:, :, 0, :], src.rearrange("p (t k) -> p t k", t=TPQ), ACT.Copy)
                elif i == PROJ_OUTS - 1:
                    ins = act.activation(vT[:], src, ACT.Copy)
                else:
                    ins = act.activation(qT_hi[:, i - 1, :], src, ACT.Copy, scale=SCALE)
                ins.then_inc(qkv_hi_done, 1)

            def pT_hi_part(u, c):
                act.wait_ge(pT_mm, u * CHUNKS + c + 1)
                act.activation(pT_hi[:, c % 2, :], ps[:, TR[c % 2], :], ACT.Copy).then_inc(pT_hi_done, 1)

            def oT_hi_part(u, k):
                act.wait_ge(pv_mm, u * QTILES + k + 1)
                act.activation(oT_hi[:, k % 3, :], ps[:, PV[k % 2], :], ACT.Copy).then_inc(oT_hi_done, 1)

            def exps(u, i):
                b, qt, heads = score_slices(i)
                act.wait_ge(scores_biased, u * SCORE_BANKS + i + 1)
                for h, _, tile, col, n in heads:
                    s = prob[:, tile, col:col + (qt + 1) * P]
                    ins = act.activation(s, s, ACT.Exp, bias=negmax[:, n:n + 1], scale=-1.0, accum_out=rowsum[:, n:n + 1])
                ins.then_inc(exp_done, 1)

            def cluster_exps(p):
                act.wait_ge(cl_max_done, p + 1)
                for j in range(TPQ):
                    ins = act.activation(cl_exp[:, j * CLUSTERS:(j + 1) * CLUSTERS],
                                         ps[:, TR[1], j * CLUSTERS:(j + 1) * CLUSTERS], ACT.Exp,
                                         bias=cl_bias[:, j:j + 1], scale=INV_TEMP, accum_out=cl_sum[:, j:j + 1])
                ins.then_inc(cl_exp_done, 1)

            def body(u, proj, attn, L=None, quad=None, p=None):
                for i in range(PROJ_OUTS):
                    if proj:
                        proj_hi(u, i)
                    if attn:
                        pT_hi_part(u, i)
                        if i in (1, 3, 4):
                            oT_hi_part(u, {1: 0, 3: 1, 4: 2}[i])
                    if L is not None:
                        if i == 1:
                            ln_root(L)
                        if i >= 4:
                            ln_hi(L, 2 * i - 8, quad)
                            ln_hi(L, 2 * i - 7, quad)
                if attn:
                    oT_hi_part(u, 3)
                if proj:
                    exps(u, 0)
                    act.wait_ge(v_mm, u + 1)
                    act.activation(v_hi[:], ps[:, TR[0], :].rearrange("p (t d) -> p t d", t=TPQ), ACT.Copy).then_inc(v_hi_done, 1)
                if p is not None:
                    cluster_exps(p)
                if proj:
                    for i in range(1, SCORE_BANKS):
                        exps(u, i)

            def first_w_hi(c):
                act.wait_ge(raw_loaded[c % 2], 48 * (c // 2 + 1))
                act.activation(wqkv_hi[:, c, :], raw[:, c % 2, :], ACT.Copy).then_inc(w_hi_done, 1)

            act.wait_ge(dist_sq, 1)
            act.activation(bias[:, 0, :], dist[:], ACT.Sqrt).then_inc(dist_sqrt, 1)
            first_w_hi(0)
            first_w_hi(1)
            ln_root(0)
            first_w_hi(2)
            first_w_hi(3)
            for j in range(TPQ):
                ln_hi(0, j, 0)
            body(0, True, False, 1, 1)
            with act.Fori(1, QUADS - 1) as u:
                body(u, True, True, u + 1, u + 1)
            with act.Fori(QUADS - 1, UNITS - 2) as u:
                body(u, True, True)
            for t in range(NC):
                act.wait_ge(wT_mm, t + 1)
                act.activation(wT_hi[:, :, t * P:(t + 1) * P], ps[:, WT_BANKS[t], :].rearrange("p (c t) -> p c t", c=NC),
                               ACT.Copy).then_inc(wT_hi_done, 1)
            act.wait_ge(wT_mm, NC + 1)
            act.wait_ge(raw_split, 2 * NC * NKV)
            act.activation(cT_hi[:], ps[:, WT_BANKS[NC], 0:NC * CLUSTERS].rearrange("p (c n) -> p c n", c=NC),
                           ACT.Copy).then_inc(wT_hi_done, 1)
            with act.Fori(UNITS - 2, UNITS) as u:
                body(u, True, True, u - (UNITS - 6), 0, u - (UNITS - 2))
            body(UNITS, False, True, 6, 0, 2)
            ln_root(7)
            for j in range(TPQ):
                ln_hi(7, j, 0)
            cluster_exps(3)

        @block.vector
        def _(dve):
            steps = [0]

            def step(ins):
                steps[0] += 1
                ins.then_inc(dve_step, 1)
                dve.wait_ge(dve_step, steps[0])

            dve.sem_inc(pT_lo_done, CHUNKS)
            dve.sem_inc(oT_lo_done, QTILES)
            dve.sem_inc(added, QTILES)

            LN_STEPS = 8

            def ln_stats(L, quad):
                for j in range(TPQ):
                    ins = dve.bn_stats(stats[:, j, :], acc[:, rows(quad, j, 1)])
                ins.then_inc(ln_step, 1)
                dve.wait_ge(ln_step, L * LN_STEPS + 1)
                dve.sem_inc(dve_marks, 1)
                for j in range(TPQ):
                    ins = dve.bn_aggr(meanvar[:, j, :], stats[:, j, :])
                ins.then_inc(ln_step, 1)
                dve.wait_ge(ln_step, L * LN_STEPS + 2)
                dve.tensor_scalar(rs[:, 0, :], meanvar[:, :, 1], LN_EPS, None, ALU.add).then_inc(var_ready, 1)

            def ln_scale(L):
                n = [2]

                def chained(ins):
                    n[0] += 1
                    ins.then_inc(ln_step, 1)
                    dve.wait_ge(ln_step, L * LN_STEPS + n[0])

                dve.wait_ge(std_ready, L + 1)
                chained(dve.reciprocal(rs[:, 2, :], rs[:, 1, :]))
                chained(dve.tensor_tensor(rs[:, 3, :], rs[:, 2, :], rs[:, 2, :], ALU.mult))
                chained(dve.tensor_tensor(rs[:, 4, :], rs[:, 3, :], rs[:, 0, :], ALU.mult))
                chained(dve.tensor_scalar(rs[:, 3, :], rs[:, 4, :], -0.5, 1.5, ALU.mult, ALU.add))
                chained(dve.tensor_copy(rs[:, 4, :], meanvar[:, :, 0]))
                chained(dve.tensor_tensor(rs[:, 5, :], rs[:, 3, :], rs[:, 2, :], ALU.mult))
                assert n[0] == LN_STEPS

            def ln_apply(L, j, quad, u=None):
                if u is not None:
                    dve.wait_ge(pT_mm, u * CHUNKS + LN_AFTER_CHUNK[j] + 1)
                if not (isinstance(L, int) and L == 0):
                    dve.wait_ge(ln_mm, L * TPQ - TPQ + j + 1)
                dve.tensor_scalar(prob[:, j, :], acc[:, rows(quad, j, 1)], rs[:, 4, j:j + 1], rs[:, 5, j:j + 1],
                                  ALU.subtract, ALU.mult).then_inc(ln_ready, 1)

            def ln_lo(L, j, quad):
                dve.wait_ge(ln_hi_done, L * TPQ + j + 1)
                dve.tensor_tensor(ln_part(quad, 1, j), ps[:, SC[j % 2], :].rearrange("p (c t) -> p c t", c=NC),
                                  ln_part(quad, 0, j).bitcast(F32), ALU.subtract).then_inc(ln_lo_done, 1)

            def proj_lo(u, i):
                dve.wait_ge(qkv_hi_done, u * PROJ_OUTS + i + 1)
                src = ps[:, PJ[i % 2], :]
                if i == 0:
                    ins = dve.tensor_tensor(kT[:, :, 1, :], src.rearrange("p (t k) -> p t k", t=TPQ),
                                            kT[:, :, 0, :].bitcast(F32), ALU.subtract)
                else:
                    ins = dve.scalar_tensor_tensor(qT_lo[:, i - 1, :], src, SCALE, qT_hi[:, i - 1, :].bitcast(F32),
                                                   ALU.mult, ALU.subtract)
                ins.then_inc(qk_lo_done, 1)

            def pT_lo_part(u, c):
                dve.wait_ge(pT_hi_done, u * CHUNKS + c + 1)
                dve.tensor_tensor(pT_lo[:, c % 2, :], ps[:, TR[c % 2], :], pT_hi[:, c % 2, :].bitcast(F32),
                                  ALU.subtract).then_inc(pT_lo_done, 1)

            def oT_lo_part(u, k):
                dve.wait_ge(oT_hi_done, u * QTILES + k + 1)
                dve.tensor_tensor(oT_lo[:, k % 3, :], ps[:, PV[k % 2], :], oT_hi[:, k % 3, :].bitcast(F32),
                                  ALU.subtract).then_inc(oT_lo_done, 1)

            def add_out(u, k):
                dve.wait_ge(wo_mm, u * QTILES + k + 1)
                at = bass.ds(quad_of(u + QUADS - 1) * (TPQ * HID) + k * HID, HID)
                dve.tensor_tensor(acc[:, at], ps[:, PJ[k % 2], :], acc[:, at], ALU.add).then_inc(added, 1)

            def add_bias(u, i):
                b, qt, heads = score_slices(i)
                if i == 0:
                    dve.wait_ge(bias_ready, group_count(u))
                dve.wait_ge(s_mm, u * SCORE_BANKS + i + 1)
                if qt == 0:
                    h0, _, tile, col, _ = heads[0]
                    dve.tensor_tensor(prob[:, tile, col:col + 2 * P].rearrange("p (h k) -> p h k", h=2),
                                      ps[:, SC[i % 2], :].rearrange("p (h s k) -> p h s k", h=2, s=2)[:, :, 1, :],
                                      bias[:, h0:h0 + 2, P:SEQ], ALU.add).then_inc(lo_biased, 1)
                    dve.wait_ge(lo_biased, u * 4 + 2 * b + i % 2 + 1)
                dve.sem_inc(dve_marks, 1)
                for h, bank_col, tile, col, n in heads:
                    s = prob[:, tile, col:col + (qt + 1) * P]
                    ins = dve.tensor_tensor_reduce(
                        out=s, in0=ps[:, SC[i % 2], bank_col:bank_col + (qt + 1) * P], in1=bias[:, h, :] if qt else s,
                        scale=-1.0, scalar=BIGGEST, op0=ALU.add, op1=ALU.min, accum_out=negmax[:, n:n + 1])
                ins.then_inc(scores_biased, 1)

            def normalise(u, i):
                b, qt, heads = score_slices(i)
                first = heads[0][4]
                dve.wait_ge(exp_done, u * SCORE_BANKS + i + 1)
                dve.reciprocal(rinv[:, first:first + 2], rowsum[:, first:first + 2]).then_inc(rinv_done, 1)
                dve.wait_ge(rinv_done, u * SCORE_BANKS + i + 1)
                for h, _, tile, col, n in heads:
                    s = prob[:, tile, col:col + (qt + 1) * P]
                    ins = dve.tensor_scalar(s, s, rinv[:, n:n + 1], None, ALU.mult)
                ins.then_inc(probs_ready, 1)

            FFN_STEPS = 4 + TPQ

            def ffn_wait(p, n):
                dve.wait_ge(ffn_step, p * FFN_STEPS + n)

            def cluster_bias(p):
                dve.wait_ge(logit_mm, p + 1)
                logits = ps[:, TR[1], 0:TPQ * CLUSTERS].rearrange("p (t c) -> p t c", t=TPQ)
                dve.tensor_reduce(cl_nmax[:], logits, AX_X, ALU.max, negate=True).then_inc(ffn_step, 1)
                ffn_wait(p, 1)
                dve.tensor_scalar(cl_bias[:], cl_nmax[:], INV_TEMP, None, ALU.mult).then_inc(cl_max_done, 1)

            def cluster_hits(p):
                dve.wait_ge(cl_exp_done, p + 2)
                dve.reciprocal(cl_rinv[:], cl_sum[:]).then_inc(ffn_step, 1)
                ffn_wait(p, 2)
                for j in range(TPQ):
                    e = cl_exp[:, j * CLUSTERS:(j + 1) * CLUSTERS]
                    ins = dve.tensor_scalar(e, e, cl_rinv[:, j:j + 1], THRESHOLD, ALU.mult, ALU.is_gt)
                ins.then_inc(ffn_step, 1)
                ffn_wait(p, 3)
                dve.tensor_reduce(query_sel[:], cl_exp[:].rearrange("p (t c) -> p t c", t=TPQ), AX_X, ALU.max)
                dve.tensor_reduce(quad_hits[:, bass.ds(p * CLUSTERS, CLUSTERS)],
                                  cl_exp[:].rearrange("p (t c) -> p c t", c=CLUSTERS), AX_X, ALU.max).then_inc(ffn_step, 1)
                ffn_wait(p, 4)

            def dense_part(p, quad, j):
                at = rows(quad, j, 1)
                dve.wait_ge(dense_mm, p * TPQ + j + 1)
                dve.tensor_tensor(selected[:, at], ps[:, PV[j % 2], :], bias_bc[:], ALU.add).then_inc(ffn_step, 1)
                ffn_wait(p, 5 + j)
                dve.scalar_tensor_tensor(selected[:, at], selected[:, at], query_sel[:, j:j + 1], acc[:, at],
                                         ALU.mult, ALU.add).then_inc(dense_out, 1)

            def body(u, proj, attn, L=None, quad=None, source=None, p=None):
                for i in range(PROJ_OUTS):
                    if proj and i < PROJ_OUTS - 1:
                        proj_lo(u, i)
                    if attn and i < 4:
                        normalise(u - 1, i + 4)
                    if attn:
                        pT_lo_part(u, i)
                        if i in (1, 3, 4):
                            oT_lo_part(u, {1: 0, 3: 1, 4: 2}[i])
                    if L is not None:
                        t_u = u if attn else None
                        if i == 0:
                            if p is not None:
                                dve.wait_ge(added, u * QTILES)
                            ln_stats(L, source)
                        elif i == 1:
                            ln_scale(L)
                            ln_apply(L, 0, source, t_u)
                        elif i == 2:
                            ln_apply(L, 1, source, t_u)
                            ln_apply(L, 2, source, t_u)
                        elif i == 3:
                            ln_apply(L, 3, source, t_u)
                        else:
                            ln_lo(L, 2 * i - 8, quad)
                            ln_lo(L, 2 * i - 7, quad)
                if attn:
                    oT_lo_part(u, 3)
                    add_out(u, 0)
                if proj:
                    add_bias(u, 0)
                    add_bias(u, 1)
                    dve.wait_ge(v_hi_done, u + 1)
                    dve.tensor_tensor(v_lo[:], ps[:, TR[0], :].rearrange("p (t d) -> p t d", t=TPQ),
                                      v_hi[:].bitcast(F32), ALU.subtract).then_inc(v_lo_done, 1)
                if p is not None:
                    cluster_bias(p)
                if attn:
                    add_out(u, 1)
                if p is not None:
                    cluster_hits(p)
                    dense_part(p, source, 0)
                if proj:
                    add_bias(u, 2)
                    add_bias(u, 3)
                    normalise(u, 0)
                    normalise(u, 1)
                if p is not None:
                    dense_part(p, source, 1)
                if attn:
                    add_out(u, 2)
                if proj:
                    add_bias(u, 4)
                    add_bias(u, 5)
                    normalise(u, 2)
                    normalise(u, 3)
                if p is not None:
                    dense_part(p, source, 2)
                if attn:
                    add_out(u, 3)
                if p is not None:
                    dense_part(p, source, 3)
                if proj:
                    add_bias(u, 6)
                    add_bias(u, 7)

            dve.sem_inc(dense_out, TPQ)
            dve.wait_ge(x_loaded[0], 16)
            ln_stats(0, 0)
            ln_scale(0)
            for j in range(TPQ):
                ln_apply(0, j, 0)
            for j in range(TPQ):
                ln_lo(0, j, 0)
            dve.wait_ge(ffn_consts, 2)
            dve.wait_ge(assign_loaded, 16)
            step(dve.tensor_copy(prob[0:CLUSTERS, 5, :], prob[0:CLUSTERS, 4, :].bitcast(I32)))
            dve.tensor_scalar(onehot[:], prob[0:CLUSTERS, 5, :], cluster_id[:], None, ALU.is_equal).then_inc(onehot_ready, 1)

            dve.wait_ge(dist_sqrt, 1)
            step(dve.reciprocal(bias[:, 1, :], bias[:, 0, :]))
            step(dve.tensor_tensor(bias[:, 2, :], bias[:, 1, :], dist[:], ALU.mult))
            step(dve.tensor_tensor(bias[:, 3, :], bias[:, 2, :], bias[:, 0, :], ALU.add))
            dve.tensor_scalar(dist[:], bias[:, 3, :], -0.5, None, ALU.mult).then_inc(dist_ready, 1)
            dve.wait_ge(x_loaded[1], 16)
            body(0, True, False, 1, 1, 1)
            dve.wait_ge(x_loaded[2], 16)
            dve.wait_ge(x_loaded[3], 16)
            with dve.Fori(1, QUADS - 1) as u:
                body(u, True, True, u + 1, u + 1, u + 1)
            with dve.Fori(QUADS - 1, UNITS - 2) as u:
                body(u, True, True)
            for t in range(NC):
                dve.wait_ge(wT_hi_done, t + 1)
                dve.tensor_tensor(wT_lo[:, :, t * P:(t + 1) * P], ps[:, WT_BANKS[t], :].rearrange("p (c t) -> p c t", c=NC),
                                  wT_hi[:, :, t * P:(t + 1) * P].bitcast(F32), ALU.subtract).then_inc(wT_lo_done, 1)
            dve.wait_ge(wT_hi_done, NC + 1)
            dve.tensor_tensor(cT_lo[:], ps[:, WT_BANKS[NC], 0:NC * CLUSTERS].rearrange("p (c n) -> p c n", c=NC),
                              cT_hi[:].bitcast(F32), ALU.subtract).then_inc(wT_lo_done, 1)
            dve.wait_ge(bias_loaded, 16)
            with dve.Fori(UNITS - 2, UNITS) as u:
                body(u, True, True, u - (UNITS - 6), 0, u - (UNITS - 2), u - (UNITS - 2))
            body(UNITS, False, True, 6, 0, 2, 2)
            dve.wait_ge(added, QTILES * (UNITS + 1))
            ln_stats(7, 3)
            ln_scale(7)
            for j in range(TPQ):
                ln_apply(7, j, 3)
            for j in range(TPQ):
                ln_lo(7, j, 0)
            cluster_bias(3)
            cluster_hits(3)
            dve.tensor_reduce(any_hit[:], quad_hits[:].rearrange("p (q c) -> p c q", c=CLUSTERS), AX_X, ALU.max).then_inc(any_ready, 1)
            dense_part(3, 3, 0)
            dve.wait_ge(sel_mm, 1)
            dve.tensor_scalar(cluster_sel[:], ps[0:CLUSTERS, PJ[0], 0:P], 0.0, None, ALU.is_gt).then_inc(csel_ready, 1)
            dense_part(3, 3, 1)
            dve.wait_ge(sel_mm, 2)

            def finish(tiles):
                for t in tiles:
                    at = slice(t * HID, (t + 1) * HID)
                    dve.copy_predicated(acc[:, at], ps[:, PJ[1], :].bitcast(I32), selected[:, at]).then_inc(final, 1)

            finish(range(0, 4))
            dense_part(3, 3, 2)
            finish(range(4, 8))
            dense_part(3, 3, 3)
            dve.wait_ge(dense_out, TPQ * (QUADS + 1))
            finish(range(8, TILES))

        @block.tensor
        def _(pe):
            def three_pass(dst, terms, start, stop):
                n = 3 * len(terms)
                m = 0
                for (l_hi, l_lo), (r_hi, r_lo) in terms:
                    for l, r in ((l_hi, r_hi), (l_hi, r_lo), (l_lo, r_hi)):
                        ins = pe.matmul(dst, l, r, start=start and m == 0, stop=stop and m == n - 1)
                        m += 1
                return ins

            pe.sem_inc(pT_mm, CHUNKS)
            pe.sem_inc(pv_mm, QTILES)
            pe.sem_inc(wo_mm, QTILES)
            pe.wait_ge(ident_ready, 1)

            def ln_transpose(L, j):
                pe.wait_ge(ln_ready, L * TPQ + j + 1)
                if not (isinstance(L, int) and L == 0 and j < 2):
                    pe.wait_ge(ln_lo_done, L * TPQ + j - 1)
                for c in range(NC):
                    ins = pe.transpose(ps[:, SC[j % 2], c * P:(c + 1) * P], prob[:, j, c * P:(c + 1) * P], ident[:])
                ins.then_inc(ln_mm, 1)

            def project(u, i):
                if i == 0:
                    pe.wait_ge(wqkv_ready, group_count(u))
                col = HPG * D if i == 0 else (HPG + 1) * D if i == PROJ_OUTS - 1 else (i - 1) * D
                flat = xnT[:].rearrange("p q s c t -> p (q s c t)")
                at = [quad_of(u) * (2 * NC * UT) + n * UT for n in range(2 * NC)]
                terms = [((wqkv_hi[:, c, col:col + D], wqkv_lo[:, c, col:col + D]),
                          (flat[:, bass.ds(at[c], UT)], flat[:, bass.ds(at[NC + c], UT)])) for c in range(NC)]
                three_pass(ps[:, PJ[i % 2], :], terms, True, True).then_inc(qkv_mm, 1)

            def transpose_probs(u, c):
                b, qt, kt, blocks = chunk_blocks(c)
                pe.wait_ge(probs_ready, u * SCORE_BANKS - SCORE_BANKS + 4 * b + 2 * qt + 2)
                for h, (bank, col) in enumerate(blocks):
                    ins = pe.transpose(ps[:, TR[c % 2], h * P:(h + 1) * P], prob[:, bank, col:col + P], ident[:])
                ins.then_inc(pT_mm, 1)

            def apply_v(u, c):
                b, qt, kt, _ = chunk_blocks(c)
                k = 2 * b + qt
                pe.wait_ge(pT_lo_done, u * CHUNKS + c + 1)
                if kt == 0:
                    pe.wait_ge(oT_lo_done, u * QTILES + k - 1)
                t = 2 * b + kt
                ins = three_pass(ps[:, PV[k % 2], :], [((v_hi[:, t, :], v_lo[:, t, :]), (pT_hi[:, c % 2, :], pT_lo[:, c % 2, :]))],
                                 kt == 0, kt == qt)
                if kt == qt:
                    ins.then_inc(pv_mm, 1)

            def project_out(u, k):
                pe.wait_ge(oT_lo_done, u * QTILES + k + 1)
                terms = [((oT_hi[:, k % 3, h * P:(h + 1) * P], oT_lo[:, k % 3, h * P:(h + 1) * P]),
                          (wo_hi[:, h, :], wo_lo[:, h, :])) for h in range(HPG)]
                three_pass(ps[:, PJ[k % 2], :], terms, True, True).then_inc(wo_mm, 1)

            def scores(u, i):
                b, qt, heads = score_slices(i)
                if not (isinstance(u, int) and i < 2):
                    pe.wait_ge(scores_biased, u * SCORE_BANKS + i - 1)
                for h, col, _, _, _ in heads:
                    q0 = b * SEQ + qt * P
                    q_hi, q_lo = qT_hi[:, h, q0:q0 + P], qT_lo[:, h, q0:q0 + P]
                    dst = ps[:, SC[i % 2], col:col + SEQ]
                    if qt == 0:
                        both = kT[:, 2 * b, :, :]
                        pe.matmul(dst, q_hi, both, start=True, stop=False)
                        ins = pe.matmul(dst, q_lo, both, start=False, stop=True)
                    else:
                        ins = three_pass(dst, [((q_hi, q_lo), (kT[:, 2 * b:2 * b + 2, 0, :], kT[:, 2 * b:2 * b + 2, 1, :]))],
                                         True, True)
                ins.then_inc(s_mm, 1)

            def cluster_logits(p, u):
                pe.wait_ge(ln_lo_done, p * TPQ + TPQ * (QUADS + 1))
                pe.wait_ge(cl_exp_done, p + 1)
                if u is not None:
                    pe.wait_ge(pT_lo_done, u * CHUNKS + CHUNKS)
                for j in range(TPQ):
                    at = slice(j * P, (j + 1) * P)
                    terms = [((x2T_hi[:, c, at], x2T_lo[:, c, at]), (cT_hi[:, c, :], cT_lo[:, c, :])) for c in range(NC)]
                    ins = three_pass(ps[:, TR[1], j * CLUSTERS:(j + 1) * CLUSTERS], terms, True, True)
                ins.then_inc(logit_mm, 1)

            def dense(p, j):
                at = slice(j * P, (j + 1) * P)
                pe.wait_ge(dense_out, p * TPQ + j + 3)
                terms = [((x2T_hi[:, c, at], x2T_lo[:, c, at]), (wT_hi[:, c, :], wT_lo[:, c, :])) for c in range(NC)]
                three_pass(ps[:, PV[j % 2], :], terms, True, True).then_inc(dense_mm, 1)

            def body(u, proj, attn, L=None, p=None):
                for i in range(PROJ_OUTS):
                    if proj:
                        if i < 2:
                            if attn:
                                pe.wait_ge(added, u * QTILES + i - 1)
                        else:
                            pe.wait_ge(qk_lo_done, u * 5 + i - 1)
                        project(u, i)
                    if attn:
                        if i == 0:
                            pe.wait_ge(v_lo_done, u)
                        else:
                            pe.wait_ge(pT_lo_done, u * CHUNKS + i - 1)
                        if i == 1 and p is not None:
                            pe.wait_ge(cl_exp_done, p + 1)
                            pe.wait_ge(dense_out, p * TPQ + TPQ)
                        transpose_probs(u, i)
                        if i > 0:
                            apply_v(u, i - 1)
                    if L is not None and i >= 4:
                        if i == 4 and attn:
                            pe.wait_ge(scores_biased, u * SCORE_BANKS)
                        ln_transpose(L, 2 * i - 8)
                        ln_transpose(L, 2 * i - 7)
                if attn:
                    if proj:
                        pe.wait_ge(qk_lo_done, u * 5 + 5)
                    else:
                        pe.wait_ge(added, u * QTILES - 1)
                    pe.wait_ge(wo_ready, group_count(u - 1))
                    project_out(u, 0)
                    apply_v(u, CHUNKS - 1)
                if proj:
                    if not attn:
                        pe.wait_ge(qk_lo_done, 5)
                    if L is not None:
                        pe.wait_ge(ln_lo_done, L * TPQ + TPQ)
                    scores(u, 0)
                    scores(u, 1)
                    pe.wait_ge(qkv_hi_done, u * PROJ_OUTS + 6)
                    pe.wait_ge(pT_lo_done, u * CHUNKS + 5)
                    for t in range(TPQ):
                        ins = pe.transpose(ps[:, TR[0], t * P:(t + 1) * P], vT[:, t * P:(t + 1) * P], ident[:])
                    ins.then_inc(v_mm, 1)
                if p is not None:
                    cluster_logits(p, u)
                if attn:
                    if not proj:
                        pe.wait_ge(added, u * QTILES)
                    project_out(u, 1)
                if p is not None:
                    pe.wait_ge(oT_lo_done, u * QTILES + QTILES)
                    dense(p, 0)
                if proj:
                    scores(u, 2)
                    scores(u, 3)
                if p is not None:
                    dense(p, 1)
                if attn:
                    pe.wait_ge(added, u * QTILES + 1)
                    project_out(u, 2)
                if proj:
                    scores(u, 4)
                    scores(u, 5)
                if p is not None:
                    dense(p, 2)
                if attn:
                    pe.wait_ge(added, u * QTILES + 2)
                    project_out(u, 3)
                if p is not None:
                    dense(p, 3)
                if proj:
                    scores(u, 6)
                    scores(u, 7)

            for j in range(TPQ):
                ln_transpose(0, j)
            pe.wait_ge(ln_lo_done, TPQ)
            body(0, True, False, 1)
            with pe.Fori(1, QUADS - 1) as u:
                pe.wait_ge(ln_lo_done, u * TPQ + TPQ)
                body(u, True, True, u + 1)
            pe.wait_ge(ln_lo_done, TPQ * QUADS)
            with pe.Fori(QUADS - 1, UNITS - 2) as u:
                body(u, True, True)
            pe.wait_ge(wc_loaded, 32)
            pe.wait_ge(scores_biased, SCORE_BANKS * (UNITS - 2))
            pe.wait_ge(oT_lo_done, QTILES * (UNITS - 2))
            pe.wait_ge(pT_lo_done, CHUNKS * (UNITS - 2))
            for t in range(NC):
                for c in range(NC):
                    ins = pe.transpose(ps[:, WT_BANKS[t], c * P:(c + 1) * P], w_raw[:, t, c * P:(c + 1) * P], ident[:])
                ins.then_inc(wT_mm, 1)
            for c in range(NC):
                ins = pe.transpose(ps[:, WT_BANKS[NC], c * CLUSTERS:(c + 1) * CLUSTERS], c_raw[:, c * P:(c + 1) * P],
                                   ident[0:CLUSTERS, 0:CLUSTERS])
            ins.then_inc(wT_mm, 1)
            pe.wait_ge(wT_lo_done, NC + 1)
            with pe.Fori(UNITS - 2, UNITS) as u:
                body(u, True, True, u - (UNITS - 6), u - (UNITS - 2))
            body(UNITS, False, True, 6, 2)
            for j in range(TPQ):
                ln_transpose(7, j)
            cluster_logits(3, None)
            dense(3, 0)
            dense(3, 1)
            pe.wait_ge(any_ready, 1)
            pe.matmul(ps[0:CLUSTERS, PJ[0], 0:P], any_hit[:], ones[:], start=True, stop=True).then_inc(sel_mm, 1)
            dense(3, 2)
            pe.wait_ge(csel_ready, 1)
            pe.wait_ge(onehot_ready, 1)
            pe.matmul(ps[:, PJ[1], :], cluster_sel[:], onehot[:], start=True, stop=True).then_inc(sel_mm, 1)
            dense(3, 3)


_INS = ['L0_attn_hidden_states', 'L0_attn_w_qkv', 'L0_attn_w_o', 'L0_ffn_weight', 'L0_ffn_bias', 'L0_ffn_centroids',
        'L0_ffn_assignments']


def kernel(**inputs):
    import numpy as np
    import concourse.bacc as bacc
    from concourse.bass_utils import run_bass_kernel_spmd

    nc = bacc.Bacc("TRN2", target_bir_lowering=False, num_devices=1)
    arrays, args = {}, []
    for name in _INS:
        a = np.ascontiguousarray(inputs[name])
        if name == 'L0_attn_hidden_states':
            a = a.reshape(TOK, HID)
        arrays[f"in_{name}"] = a
        args.append(nc.dram_tensor(f"in_{name}", a.shape, mybir.dt.from_np(a.dtype), kind="ExternalInput").ap())
    args.append(nc.dram_tensor("out", [TOK, HID], F32, kind="ExternalOutput").ap())
    build(nc, *args)
    r = run_bass_kernel_spmd(nc, [arrays], core_ids=[0])
    return r.results[0]["out"].reshape(BATCH, SEQ, HID)
```

```python
from contextlib import ExitStack

import concourse.bass as bass
from concourse import mybir

ALU = mybir.AluOpType
ACT = mybir.ActivationFunctionType
F32 = mybir.dt.float32
F32R = mybir.dt.float32r
BF16 = mybir.dt.bfloat16
I32 = mybir.dt.int32
AX_X = mybir.AxisListType.X

P = 128
BATCH, SEQ, HID = 8, 256, 512
NH, NKV, D = 32, 8, 128
HPG = NH // NKV
TOK = BATCH * SEQ
TILES = TOK // P
NC = HID // P
UT = 512
QUADS = TOK // UT
TPQ = UT // P
UNITS = NKV * QUADS
QKV_W = (HPG + 2) * D
SCALE = float(D) ** -0.5
LN_EPS = 1e-5
MASKED = -3.0e38
BIGGEST = 3.0e38
CLUSTERS = 64
INV_TEMP = 1.0 / 0.10000000149011612
THRESHOLD = 0.01
ALIBI_BASE = 2.0 ** (-8.0 / NH)

PROJ_OUTS = 6
CHUNKS = 6
SCORE_BANKS = 8
PROB_TILES = 6
QTILES = 4


def build(nc, x_in, w_qkv, w_o, w_ffn, b_ffn, cents, assign, out):
    ctx = ExitStack()
    with ctx:
        def sem(name):
            return ctx.enter_context(nc.semaphore(name))

        def sb(name, shape, dt, where=ctx):
            return where.enter_context(nc.sbuf_tensor(name, shape, dt))

        acc = sb("acc", [P, TILES * HID], F32)
        ident = sb("ident", [P, P], F32)
        fold = sb("fold", [P, CLUSTERS], F32)
        stats = sb("stats", [P, TPQ, 6], F32)
        meanvar = sb("meanvar", [P, TPQ, 2], F32)
        rs = sb("rs", [P, 6, TPQ], F32)
        onehot = sb("onehot", [CLUSTERS, HID], BF16)
        ones = sb("ones", [P, P], BF16)
        cluster_id = sb("cluster_id", [CLUSTERS, 1], F32)
        cl_nmax = sb("cl_nmax", [P, TPQ], F32)
        cl_bias = sb("cl_bias", [P, TPQ], F32)
        cl_sum = sb("cl_sum", [P, TPQ], F32)
        cl_rinv = sb("cl_rinv", [P, TPQ], F32)
        query_sel = sb("query_sel", [P, 2, TPQ], F32)

        att = ExitStack()
        xnT = sb("xnT", [P, QUADS, 2, NC, UT], F32R, att)
        raw = sb("raw", [P, 2, QKV_W], F32, att)
        wqkv_hi = sb("wqkv_hi", [P, NC, QKV_W], F32R, att)
        wqkv_lo = sb("wqkv_lo", [P, NC, QKV_W], F32R, att)
        wo_hi = sb("wo_hi", [P, HPG, HID], F32R, att)
        wo_lo = sb("wo_lo", [P, HPG, HID], F32R, att)
        qT_hi = sb("qT_hi", [P, HPG, UT], F32R, att)
        qT_lo = sb("qT_lo", [P, HPG, UT], F32R, att)
        kT = sb("kT", [P, TPQ, 2, P], F32R, att)
        vT = sb("vT", [P, UT], F32, att)
        v_hi = sb("v_hi", [P, TPQ, D], F32R, att)
        v_lo = sb("v_lo", [P, TPQ, D], F32R, att)
        prob = sb("prob", [P, PROB_TILES, 512], F32, att)
        pT_hi = sb("pT_hi", [P, 2, 512], F32R, att)
        pT_lo = sb("pT_lo", [P, 2, 512], F32R, att)
        oT_hi = sb("oT_hi", [P, 3, 512], F32R, att)
        oT_lo = sb("oT_lo", [P, 3, 512], F32R, att)
        bias = sb("bias", [P, HPG, SEQ], F32, att)
        dist = sb("dist", [P, SEQ], F32, att)
        negmax = sb("negmax", [P, 16], F32, att)
        rowsum = sb("rowsum", [P, 16], F32, att)
        rinv = sb("rinv", [P, 16], F32, att)
        att.close()

        x2T_hi, x2T_lo = xnT[:, 0, 0], xnT[:, 0, 1]
        wT_hi, wT_lo = xnT[:, 1, 0], xnT[:, 1, 1]
        logitT = vT
        cl_exp = dist
        x3T_hi, x3T_lo = wqkv_hi[:, :, 0:UT], wqkv_lo[:, :, 0:UT]
        LAST = -1

        ffn = ExitStack()
        w_raw = sb("w_raw", [P, NC, HID], F32, ffn)
        c_raw = sb("c_raw", [CLUSTERS, HID], F32, ffn)
        sb("gap", [P, 22 * 256], F32, ffn)
        selected = sb("selected", [P, TILES * HID], F32, ffn)
        cT = sb("cT", [P, NC, 2, CLUSTERS], F32R, ffn)
        bias_bc = sb("bias_bc", [P, HID], F32, ffn)
        quad_hits = sb("quad_hits", [P, QUADS * CLUSTERS], BF16, ffn)
        any_hit = sb("any_hit", [P, CLUSTERS], BF16, ffn)
        cluster_sel = sb("cluster_sel", [CLUSTERS, P], BF16, ffn)
        ffn.close()

        ps = ctx.enter_context(nc.psum_tensor("ps", [P, 8, 512], F32))
        PJ = (0, 1)
        TR = (2, 3)
        PV = (4, 5)
        SC = (6, 7)

        tile_loaded = [sem(f"tile_loaded{t}") for t in range(TPQ)]
        x_loaded = [None] + [sem(f"x_loaded{q}") for q in range(1, QUADS)]
        first_loaded = [sem(f"first_loaded{c}") for c in range(NC)]
        raw_loaded = [sem("raw_loaded0"), sem("raw_loaded1")]
        assign_loaded = sem("assign_loaded")
        wc_loaded = sem("wc_loaded")
        bias_loaded = sem("bias_loaded")
        stored = sem("stored")
        pool_step = sem("pool_step")
        pool_marks = sem("pool_marks")
        ident_ready = sem("ident_ready")
        dist_sq = sem("dist_sq")
        raw_split = sem("raw_split")
        wqkv_ready = sem("wqkv_ready")
        wo_ready = sem("wo_ready")
        bias_ready = sem("bias_ready")
        ffn_consts = sem("ffn_consts")
        bias_scaled = sem("bias_scaled")
        bias_added = sem("bias_added")
        ln_mm = sem("ln_mm")
        qkv_mm = sem("qkv_mm")
        pT_mm = sem("pT_mm")
        pv_mm = sem("pv_mm")
        wo_mm = sem("wo_mm")
        s_mm = sem("s_mm")
        v_mm = sem("v_mm")
        wT_mm = sem("wT_mm")
        logitT_mm = sem("logitT_mm")
        logit_mm = sem("logit_mm")
        dense_mm = sem("dense_mm")
        sel_mm = sem("sel_mm")
        w_hi_done = sem("w_hi_done")
        dist_sqrt = sem("dist_sqrt")
        std_ready = sem("std_ready")
        ln_hi_done = sem("ln_hi_done")
        qkv_hi_done = sem("qkv_hi_done")
        pT_hi_done = sem("pT_hi_done")
        oT_hi_done = sem("oT_hi_done")
        exp_done = sem("exp_done")
        v_hi_done = sem("v_hi_done")
        wT_hi_done = sem("wT_hi_done")
        logitT_copied = sem("logitT_copied")
        cl_exp_done = sem("cl_exp_done")
        dve_step = sem("dve_step")
        w_last_lo = sem("w_last_lo")
        dist_ready = sem("dist_ready")
        var_ready = sem("var_ready")
        ln_step = sem("ln_step")
        ln_ready = sem("ln_ready")
        ln_lo_done = sem("ln_lo_done")
        ffn_step = sem("ffn_step")
        onehot_ready = sem("onehot_ready")
        qk_lo_done = sem("qk_lo_done")
        pT_lo_done = sem("pT_lo_done")
        oT_lo_done = sem("oT_lo_done")
        scores_biased = sem("scores_biased")
        lo_biased = sem("lo_biased")
        dve_marks = sem("dve_marks")
        rinv_done = sem("rinv_done")
        probs_ready = sem("probs_ready")
        v_lo_done = sem("v_lo_done")
        added = sem("added")
        wT_lo_done = sem("wT_lo_done")
        cl_max_done = sem("cl_max_done")
        hits_done = sem("hits_done")
        dense_out = sem("dense_out")
        any_ready = sem("any_ready")
        csel_ready = sem("csel_ready")
        final = sem("final")

        block = ctx.enter_context(nc.Block())

        WT_BANKS = (PV[0], PV[1], TR[1], SC[0], SC[1])

        def first_raw(c):
            at = (QUADS - 1) * TPQ * HID + (c - 2) * QKV_W
            return raw[:, c, :] if c < 2 else acc[:, at:at + QKV_W]

        def group_count(u):
            return (u + QUADS) >> 2

        def quad_of(u):
            return u % QUADS

        LN_STEPS = 6
        FFN_STEPS = 4

        def selects(p):
            return query_sel[:, int(p == QUADS - 1), :]

        def own_banks(L):
            return isinstance(L, int) and L in (0, 1, 6, 7)

        def ln_bank(L, j):
            if own_banks(L):
                return {0: (SC[0], SC[1], PV[0], PV[1]), 1: (SC[0], SC[1], PV[0], PV[1]),
                        6: (TR[0], TR[1], PV[0], PV[1]), 7: (TR[0], PJ[1], PV[0], PV[1])}[L][j]
            return SC[j % 2]

        def logit_bank(p):
            return TR[0] if p == QUADS - 1 else TR[1]

        FFN_TAIL = TPQ + 2

        def dense_bank(p, j):
            n = p * TPQ + j
            if n >= FFN_TAIL:
                return (PJ[0], SC[0], SC[1], PJ[0], SC[0], TR[1], SC[1], PJ[0], PV[0], PV[1])[n - FFN_TAIL]
            return PV[j % 2]

        def out_bank(u, k):
            return (PJ[1], SC[1], PJ[0], SC[0])[k] if isinstance(u, int) and u == UNITS else PJ[k % 2]

        FIRST_SC = (TR[1], SC[0], SC[1], PV[0], PV[1])

        def is_first(u):
            return isinstance(u, int) and u == 0

        def score_bank(u, i):
            return FIRST_SC[i % len(FIRST_SC)] if is_first(u) else SC[i % 2]

        MASK_BANK = PJ[1]
        STORES = ((0, 4), (4, 4), (8, 4), (12, 2), (14, 1), (15, 1))

        def rows(q, j=0, n=TPQ):
            return bass.ds(q * (TPQ * HID) + j * HID, n * HID)

        def ffn_x(p):
            return (x3T_hi, x3T_lo) if p == QUADS - 1 else (x2T_hi, x2T_lo)

        def ln_part(quad, part, j):
            if isinstance(quad, int) and quad == LAST:
                return (x3T_hi, x3T_lo)[part][:, :, j * P:(j + 1) * P]
            if isinstance(quad, int):
                return xnT[:, quad, part, :, j * P:(j + 1) * P]
            flat = xnT[:].rearrange("p q s c t -> p (q s c t)")
            at = quad * (2 * NC * UT) + part * (NC * UT)
            return flat[:, bass.ds(at, NC * UT)].rearrange("p (c t) -> p c t", c=NC)[:, :, j * P:(j + 1) * P]

        LN_AFTER_CHUNK = (0, 2, 2, 3)

        def score_slices(i):
            b, qt, pair = i // 4, i // 2 % 2, i % 2
            heads = (2 * pair, 2 * pair + 1)
            if qt == 0:
                return b, qt, [(h, (h % 2) * SEQ, 3 * b, h * P, 8 * b + h) for h in heads]
            return b, qt, [(h, (h % 2) * SEQ, 3 * b + 1 + pair, (h % 2) * SEQ, 8 * b + HPG + h) for h in heads]

        def chunk_blocks(c):
            b, part = c // 3, c % 3
            if part == 0:
                return b, 0, 0, [(3 * b, h * P) for h in range(HPG)]
            kt = part - 1
            return b, 1, kt, [(3 * b + 1 + h // 2, (h % 2) * SEQ + kt * P) for h in range(HPG)]

        @block.sync
        def _(sp):
            def load_qkv(g, c):
                rows = w_qkv[c * P:(c + 1) * P, :]
                slot = first_raw(c) if isinstance(g, int) else raw[:, c % 2, :]
                done = first_loaded[c] if isinstance(g, int) else raw_loaded[c % 2]
                sp.dma_start(slot[:, 0:HPG * D], rows[:, bass.ds(g * (HPG * D), HPG * D)]).then_inc(done, 16)
                sp.dma_start(slot[:, HPG * D:HPG * D + D], rows[:, bass.ds(g * D + NH * D, D)]).then_inc(done, 16)
                sp.dma_start(slot[:, HPG * D + D:QKV_W], rows[:, bass.ds(g * D + (NH + NKV) * D, D)]).then_inc(done, 16)

            def load_o(g, h):
                rows = w_o[bass.ds(g * (HPG * D) + h * D, D), :]
                sp.dma_start(raw[:, h % 2, 0:HID], rows).then_inc(raw_loaded[h % 2], 16)

            def load_group(g):
                for n in range(2 * NC):
                    sp.wait_ge(raw_split, g * (2 * NC) + n - 1)
                    load_qkv(g, n) if n < NC else load_o(g, n - NC)

            def load_x(q):
                sp.dma_start(acc[:, q * TPQ * HID:(q + 1) * TPQ * HID].rearrange("p (t d) -> p t d", t=TPQ),
                             x_in[q * UT:(q + 1) * UT, :].rearrange("(t p) d -> p t d", p=P)).then_inc(x_loaded[q], 16)

            for t in range(TPQ):
                sp.dma_start(acc[:, t * HID:(t + 1) * HID], x_in[t * P:(t + 1) * P, :]).then_inc(tile_loaded[t], 16)
            for c in range(NC):
                load_qkv(0, c)
            sp.dma_start(prob[0:CLUSTERS, 4, :].bitcast(I32),
                         assign.rearrange("(a n) -> a n", a=1).broadcast_to([CLUSTERS, HID])).then_inc(assign_loaded, 16)
            load_x(1)
            load_x(2)
            for h in range(HPG):
                sp.wait_ge(raw_split, h + 1 if h < 2 else NC + h - 1)
                load_o(0, h)
            load_x(3)
            with sp.Fori(1, NKV) as g:
                load_group(g)
            sp.wait_ge(qkv_mm, PROJ_OUTS * (UNITS - QUADS + 1))
            sp.dma_start(w_raw[:], w_ffn.rearrange("(t p) d -> p t d", p=P)).then_inc(wc_loaded, 16)
            sp.dma_start(c_raw[:], cents).then_inc(wc_loaded, 16)
            sp.wait_ge(raw_split, 2 * NC * NKV)
            sp.dma_start(bias_bc[:], b_ffn.rearrange("(a n) -> a n", a=1).broadcast_to([P, HID])).then_inc(bias_loaded, 16)
            for t, n in STORES:
                sp.wait_ge(final, t + n)
                sp.dma_start(out[t * P:(t + n) * P, :].rearrange("(t p) d -> p t d", p=P),
                             acc[:, t * HID:(t + n) * HID].rearrange("p (t d) -> p t d", t=n)).then_inc(stored, 16)
            sp.wait_ge(stored, 16 * len(STORES))

        @block.gpsimd
        def _(pool):
            pool.memset(ident[:], 0.0).then_inc(pool_step, 1)
            pool.memset(ones[:], 1.0).then_inc(ffn_consts, 1)
            pool.iota(cluster_id[:], [[0, 1]], base=0, channel_multiplier=1,
                      allow_small_or_imprecise_dtypes=True).then_inc(ffn_consts, 1)
            pool.iota(dist[:], [[-1, SEQ]], base=P, channel_multiplier=1,
                      allow_small_or_imprecise_dtypes=True).then_inc(pool_step, 1)
            pool.wait_ge(pool_step, 2)
            pool.affine_select(out=ident[:], in_=ident[:], compare_op=ALU.not_equal, fill=1.0, base=0,
                               pattern=[[-1, P]], channel_multiplier=1).then_inc(ident_ready, 1)
            pool.tensor_scalar(dist[:], dist[:], 1.0, None, ALU.max).then_inc(dist_sq, 1)
            pool.wait_ge(ident_ready, 1)
            pool.tensor_tensor(fold[:], ident[:, 0:CLUSTERS], ident[:, CLUSTERS:P], ALU.add).then_inc(ffn_consts, 1)

            def split(source, hi, lo, count):
                pool.sem_inc(pool_marks, 1)
                if count is not None:
                    pool.tensor_scalar(hi, source, 1.0, 1.0, ALU.mult, ALU.mult).then_inc(pool_step, 1)
                    pool.wait_ge(pool_step, count)
                pool.tensor_tensor(lo, source, hi.bitcast(F32), ALU.subtract).then_inc(raw_split, 1)

            def split_qkv(g):
                for c in range(NC):
                    pool.wait_ge(raw_loaded[c % 2], g * 128 - 96 + 48 * (c // 2 + 1))
                    split(raw[:, c % 2, :], wqkv_hi[:, c, :], wqkv_lo[:, c, :], g * (2 * NC) + SETUP + c + 1)
                pool.wait_ge(raw_split, g * (2 * NC) + NC)
                pool.sem_inc(wqkv_ready, 1)

            def split_o(g):
                for h in range(HPG):
                    pool.wait_ge(raw_loaded[h % 2], g * 128 + 16 * (h // 2 + 1))
                    split(raw[:, h % 2, 0:HID], wo_hi[:, h, :], wo_lo[:, h, :], g * (2 * NC) + SETUP + NC + h + 1)
                pool.wait_ge(raw_split, g * (2 * NC) + 2 * NC)
                pool.sem_inc(wo_ready, 1)

            SETUP = 2 - NC
            for c in range(NC - 1):
                pool.wait_ge(w_hi_done, c + 1)
                split(first_raw(c), wqkv_hi[:, c, :], wqkv_lo[:, c, :], None)
            pool.wait_ge(raw_split, NC - 1)
            pool.wait_ge(w_last_lo, 1)
            pool.sem_inc(raw_split, 1)
            pool.sem_inc(wqkv_ready, 1)
            pool.wait_ge(dist_ready, 1)
            pool.affine_select(out=dist[:], in_=dist[:], compare_op=ALU.not_equal, fill=0.0, base=P,
                               pattern=[[-1, SEQ]], channel_multiplier=1).then_inc(dist_sq, 1)
            pool.wait_ge(dist_sq, 2)
            pool.affine_select(out=dist[:], in_=dist[:], compare_op=ALU.is_ge, fill=MASKED, base=P,
                               pattern=[[-1, SEQ]], channel_multiplier=1).then_inc(dist_sq, 1)
            pool.wait_ge(dist_sq, 3)
            for h in range(HPG):
                i = pool.tensor_scalar(bias[:, h, :], dist[:], ALIBI_BASE ** (h + 1), 1.0, ALU.mult, ALU.mult)
                i.then_inc(dist_sq, 1)
            pool.wait_ge(dist_sq, 3 + HPG)
            pool.sem_inc(bias_ready, 1)
            split_o(0)
            with pool.Fori(1, NKV) as g:
                pool.wait_ge(qkv_mm, g * (PROJ_OUTS * QUADS))
                split_qkv(g)
                pool.wait_ge(scores_biased, g * (SCORE_BANKS * QUADS))
                pool.sem_inc(pool_marks, 1)
                pool.tensor_scalar(bias[:], bias[:], ALIBI_BASE ** HPG, 1.0, ALU.mult, ALU.mult).then_inc(bias_ready, 1)
                pool.wait_ge(wo_mm, g * (4 * QUADS) + 4)
                split_o(g)
            pool.wait_ge(bias_loaded, 16)
            for p in range(QUADS):
                for j in range(TPQ):
                    at = rows(p, j, 1)
                    if p < 2:
                        pool.wait_ge(hits_done, p + 1)
                        pool.tensor_scalar(selected[:, at], bias_bc[:], selects(p)[:, j:j + 1], 1.0, ALU.mult,
                                           ALU.mult).then_inc(bias_scaled, 1)
                    pool.wait_ge(bias_scaled, p * TPQ + j + 1)
                    pool.tensor_tensor(selected[:, at], selected[:, at], acc[:, at], ALU.add).then_inc(bias_added, 1)

        @block.scalar
        def _(act):
            act.sem_inc(pT_hi_done, CHUNKS)
            act.sem_inc(oT_hi_done, QTILES)
            act.sem_inc(cl_exp_done, 1)
            def ln_root(L):
                act.wait_ge(var_ready, L + 1)
                act.activation(rs[:, 1, :], rs[:, 0, :], ACT.Sqrt).then_inc(std_ready, 1)

            def ln_hi(L, j, quad):
                act.wait_ge(ln_mm, L * TPQ + j + 1)
                act.activation(ln_part(quad, 0, j), ps[:, ln_bank(L, j), :].rearrange("p (c t) -> p c t", c=NC),
                               ACT.Copy).then_inc(ln_hi_done, 1)

            def proj_hi(u, i):
                act.wait_ge(qkv_mm, u * PROJ_OUTS + i + 1)
                src = ps[:, PJ[i % 2], :]
                if i == 0:
                    ins = act.activation(kT[:, :, 0, :], src.rearrange("p (t k) -> p t k", t=TPQ), ACT.Copy)
                elif i == PROJ_OUTS - 1:
                    ins = act.activation(vT[:], src, ACT.Copy)
                else:
                    ins = act.activation(qT_hi[:, i - 1, :], src, ACT.Copy, scale=SCALE)
                ins.then_inc(qkv_hi_done, 1)

            def pT_hi_part(u, c):
                act.wait_ge(pT_mm, u * CHUNKS + c + 1)
                act.activation(pT_hi[:, c % 2, :], ps[:, TR[c % 2], :], ACT.Copy).then_inc(pT_hi_done, 1)

            def oT_hi_part(u, k):
                act.wait_ge(pv_mm, u * QTILES + k + 1)
                act.activation(oT_hi[:, k % 3, :], ps[:, PV[k % 2], :], ACT.Copy).then_inc(oT_hi_done, 1)

            def exps(u, i):
                b, qt, heads = score_slices(i)
                act.wait_ge(scores_biased, u * SCORE_BANKS + i + 1)
                for h, _, tile, col, n in heads:
                    s = prob[:, tile, col:col + (qt + 1) * P]
                    ins = act.activation(s, s, ACT.Exp, bias=negmax[:, n:n + 1], scale=-1.0, accum_out=rowsum[:, n:n + 1])
                ins.then_inc(exp_done, 1)

            def copy_logits(p):
                act.wait_ge(logitT_mm, p + 1)
                act.activation(logitT[:], ps[:, logit_bank(p), :], ACT.Copy).then_inc(logitT_copied, 1)

            def cluster_exps(p):
                act.wait_ge(cl_max_done, p + 1)
                for j in range(TPQ):
                    at = slice(j * CLUSTERS, (j + 1) * CLUSTERS)
                    ins = act.activation(cl_exp[:, at], ps[:, logit_bank(p), at], ACT.Exp,
                                         bias=cl_bias[:, j:j + 1], scale=INV_TEMP, accum_out=cl_sum[:, j:j + 1])
                ins.then_inc(cl_exp_done, 1)

            def scaled_bias(p):
                act.wait_ge(hits_done, p + 1)
                for j in range(TPQ):
                    act.activation(selected[:, rows(p, j, 1)], bias_bc[:], ACT.Copy,
                                   scale=selects(p)[:, j:j + 1]).then_inc(bias_scaled, 1)

            def body(u, proj, attn, L=None, quad=None, p=None):
                for i in range(PROJ_OUTS):
                    if proj:
                        proj_hi(u, i)
                    if attn:
                        pT_hi_part(u, i)
                        if i < 2:
                            exps(u - 1, SCORE_BANKS - 2 + i)
                        if i in (1, 3, 4):
                            oT_hi_part(u, {1: 0, 3: 1, 4: 2}[i])
                    if L is not None:
                        if i == 2:
                            ln_root(L)
                        if i >= 4:
                            ln_hi(L, 2 * i - 8, quad)
                            ln_hi(L, 2 * i - 7, quad)
                if attn:
                    oT_hi_part(u, 3)
                if proj:
                    exps(u, 0)
                    act.wait_ge(v_mm, u + 1)
                    act.activation(v_hi[:], ps[:, TR[0], :].rearrange("p (t d) -> p t d", t=TPQ), ACT.Copy).then_inc(v_hi_done, 1)
                if p is not None:
                    copy_logits(p)
                if proj:
                    for i in range(1, SCORE_BANKS - 2):
                        exps(u, i)
                        if i == 1 and p is not None:
                            cluster_exps(p)

            def first_w_hi(c):
                act.wait_ge(first_loaded[c], 48)
                act.activation(wqkv_hi[:, c, :], first_raw(c), ACT.Copy).then_inc(w_hi_done, 1)

            act.wait_ge(dist_sq, 1)
            act.activation(bias[:, 0, :], dist[:], ACT.Sqrt).then_inc(dist_sqrt, 1)
            ln_root(0)
            first_w_hi(0)
            first_w_hi(1)
            ln_hi(0, 0, 0)
            ln_hi(0, 1, 0)
            first_w_hi(2)
            ln_hi(0, 2, 0)
            ln_hi(0, 3, 0)
            first_w_hi(3)
            body(0, True, False, 1, 1)
            with act.Fori(1, QUADS - 1) as u:
                body(u, True, True, u + 1, u + 1)
            with act.Fori(QUADS - 1, UNITS - 2) as u:
                body(u, True, True)
            for t in range(NC):
                act.wait_ge(wT_mm, t + 1)
                act.activation(wT_hi[:, :, t * P:(t + 1) * P], ps[:, WT_BANKS[t], :].rearrange("p (c t) -> p c t", c=NC),
                               ACT.Copy).then_inc(wT_hi_done, 1)
            act.wait_ge(wT_mm, NC + 1)
            act.wait_ge(raw_split, 2 * NC * NKV)
            act.activation(cT[:, :, 0, :], ps[:, WT_BANKS[NC], 0:NC * CLUSTERS].rearrange("p (c n) -> p c n", c=NC),
                           ACT.Copy).then_inc(wT_hi_done, 1)
            body(UNITS - 2, True, True, 4, 0, 0)
            body(UNITS - 1, True, True, 5, 0, 1)
            u = UNITS
            pT_hi_part(u, 0)
            pT_hi_part(u, 1)
            oT_hi_part(u, 0)
            exps(u - 1, 6)
            pT_hi_part(u, 2)
            pT_hi_part(u, 3)
            exps(u - 1, 7)
            oT_hi_part(u, 1)
            ln_root(6)
            pT_hi_part(u, 4)
            oT_hi_part(u, 2)
            pT_hi_part(u, 5)
            oT_hi_part(u, 3)
            for j in range(TPQ):
                ln_hi(6, j, 0)
            copy_logits(2)
            ln_root(7)
            for j in range(TPQ):
                ln_hi(7, j, LAST)
            cluster_exps(2)
            copy_logits(3)
            scaled_bias(2)
            cluster_exps(3)
            scaled_bias(3)

        @block.vector
        def _(dve):
            steps = [0]

            def step(ins):
                steps[0] += 1
                ins.then_inc(dve_step, 1)
                dve.wait_ge(dve_step, steps[0])

            dve.sem_inc(pT_lo_done, CHUNKS)
            dve.sem_inc(oT_lo_done, QTILES)
            dve.sem_inc(added, QTILES)

            def ln_stats_of(L, quad, j):
                ins = dve.bn_stats(stats[:, j, :], acc[:, rows(quad, j, 1)])
                if j == TPQ - 1:
                    ins.then_inc(ln_step, 1)

            def ln_var(L):
                dve.wait_ge(ln_step, L * LN_STEPS + 1)
                dve.sem_inc(dve_marks, 1)
                for j in range(TPQ):
                    ins = dve.bn_aggr(meanvar[:, j, :], stats[:, j, :])
                ins.then_inc(ln_step, 1)
                dve.wait_ge(ln_step, L * LN_STEPS + 2)
                dve.tensor_scalar(rs[:, 0, :], meanvar[:, :, 1], LN_EPS, None, ALU.add).then_inc(var_ready, 1)

            def ln_scale(L):
                n = [2]

                def chained(ins):
                    n[0] += 1
                    ins.then_inc(ln_step, 1)
                    dve.wait_ge(ln_step, L * LN_STEPS + n[0])

                dve.wait_ge(std_ready, L + 1)
                chained(dve.reciprocal(rs[:, 2, :], rs[:, 1, :]))
                chained(dve.tensor_tensor(rs[:, 3, :], rs[:, 2, :], rs[:, 0, :], ALU.mult))
                chained(dve.scalar_tensor_tensor(rs[:, 4, :], rs[:, 3, :], -0.5, rs[:, 2, :], ALU.mult, ALU.mult))
                chained(dve.scalar_tensor_tensor(rs[:, 5, :], rs[:, 4, :], 1.5, rs[:, 2, :], ALU.add, ALU.mult))
                assert n[0] == LN_STEPS

            def ln_apply(L, j, quad, u=None):
                if u is not None:
                    dve.wait_ge(pT_mm, u * CHUNKS + LN_AFTER_CHUNK[j] + 1)
                if not (isinstance(L, int) and L == 0):
                    dve.wait_ge(ln_mm, L * TPQ - TPQ + j + 1)
                dve.tensor_scalar(prob[:, j, :], acc[:, rows(quad, j, 1)], meanvar[:, j, 0:1], rs[:, 5, j:j + 1],
                                  ALU.subtract, ALU.mult).then_inc(ln_ready, 1)

            def ln_lo(L, j, quad):
                dve.wait_ge(ln_hi_done, L * TPQ + j + 1)
                dve.tensor_tensor(ln_part(quad, 1, j), ps[:, ln_bank(L, j), :].rearrange("p (c t) -> p c t", c=NC),
                                  ln_part(quad, 0, j).bitcast(F32), ALU.subtract).then_inc(ln_lo_done, 1)

            def proj_lo(u, i):
                dve.wait_ge(qkv_hi_done, u * PROJ_OUTS + i + 1)
                src = ps[:, PJ[i % 2], :]
                if i == 0:
                    ins = dve.tensor_tensor(kT[:, :, 1, :], src.rearrange("p (t k) -> p t k", t=TPQ),
                                            kT[:, :, 0, :].bitcast(F32), ALU.subtract)
                else:
                    ins = dve.scalar_tensor_tensor(qT_lo[:, i - 1, :], src, SCALE, qT_hi[:, i - 1, :].bitcast(F32),
                                                   ALU.mult, ALU.subtract)
                ins.then_inc(qk_lo_done, 1)

            def pT_lo_part(u, c):
                dve.wait_ge(pT_hi_done, u * CHUNKS + c + 1)
                dve.tensor_tensor(pT_lo[:, c % 2, :], ps[:, TR[c % 2], :], pT_hi[:, c % 2, :].bitcast(F32),
                                  ALU.subtract).then_inc(pT_lo_done, 1)

            def oT_lo_part(u, k):
                dve.wait_ge(oT_hi_done, u * QTILES + k + 1)
                dve.tensor_tensor(oT_lo[:, k % 3, :], ps[:, PV[k % 2], :], oT_hi[:, k % 3, :].bitcast(F32),
                                  ALU.subtract).then_inc(oT_lo_done, 1)

            def add_out(u, k):
                dve.wait_ge(wo_mm, u * QTILES + k + 1)
                at = bass.ds(quad_of(u + QUADS - 1) * (TPQ * HID) + k * HID, HID)
                dve.tensor_tensor(acc[:, at], ps[:, out_bank(u, k), :], acc[:, at], ALU.add).then_inc(added, 1)

            def add_bias(u, i):
                b, qt, heads = score_slices(i)
                if i == 0:
                    dve.wait_ge(bias_ready, group_count(u))
                dve.wait_ge(s_mm, u * SCORE_BANKS + i + 1)
                if qt == 0:
                    h0, _, tile, col, _ = heads[0]
                    dve.tensor_tensor(prob[:, tile, col:col + 2 * P].rearrange("p (h k) -> p h k", h=2),
                                      ps[:, score_bank(u, i), :].rearrange("p (h s k) -> p h s k", h=2, s=2)[:, :, 1, :],
                                      bias[:, h0:h0 + 2, P:SEQ], ALU.add).then_inc(lo_biased, 1)
                    dve.wait_ge(lo_biased, u * 4 + 2 * b + i % 2 + 1)
                dve.sem_inc(dve_marks, 1)
                for h, bank_col, tile, col, n in heads:
                    s = prob[:, tile, col:col + (qt + 1) * P]
                    ins = dve.tensor_tensor_reduce(
                        out=s, in0=ps[:, score_bank(u, i), bank_col:bank_col + (qt + 1) * P], in1=bias[:, h, :] if qt else s,
                        scale=-1.0, scalar=BIGGEST, op0=ALU.add, op1=ALU.min, accum_out=negmax[:, n:n + 1])
                ins.then_inc(scores_biased, 1)

            def normalise(u, i):
                b, qt, heads = score_slices(i)
                first = heads[0][4]
                dve.wait_ge(exp_done, u * SCORE_BANKS + i + 1)
                dve.reciprocal(rinv[:, first:first + 2], rowsum[:, first:first + 2]).then_inc(rinv_done, 1)
                dve.wait_ge(rinv_done, u * SCORE_BANKS + i + 1)
                for h, _, tile, col, n in heads:
                    s = prob[:, tile, col:col + (qt + 1) * P]
                    ins = dve.tensor_scalar(s, s, rinv[:, n:n + 1], None, ALU.mult)
                ins.then_inc(probs_ready, 1)

            def ffn_wait(p, n):
                dve.wait_ge(ffn_step, p * FFN_STEPS + n)

            def cluster_bias(p):
                dve.wait_ge(logit_mm, p + 1)
                logits = ps[:, logit_bank(p), 0:TPQ * CLUSTERS].rearrange("p (t c) -> p t c", t=TPQ)
                dve.tensor_reduce(cl_nmax[:], logits, AX_X, ALU.max, negate=True).then_inc(ffn_step, 1)
                ffn_wait(p, 1)
                dve.tensor_scalar(cl_bias[:], cl_nmax[:], INV_TEMP, None, ALU.mult).then_inc(cl_max_done, 1)

            def cluster_hits(p):
                dve.wait_ge(cl_exp_done, p + 2)
                dve.reciprocal(cl_rinv[:], cl_sum[:]).then_inc(ffn_step, 1)
                ffn_wait(p, 2)
                for j in range(TPQ):
                    e = cl_exp[:, j * CLUSTERS:(j + 1) * CLUSTERS]
                    ins = dve.tensor_scalar(e, e, cl_rinv[:, j:j + 1], THRESHOLD, ALU.mult, ALU.is_gt)
                ins.then_inc(ffn_step, 1)
                ffn_wait(p, 3)
                dve.tensor_reduce(selects(p), cl_exp[:].rearrange("p (t c) -> p t c", t=TPQ), AX_X, ALU.max)
                dve.tensor_reduce(quad_hits[:, bass.ds(p * CLUSTERS, CLUSTERS)],
                                  cl_exp[:].rearrange("p (t c) -> p c t", c=CLUSTERS), AX_X, ALU.max).then_inc(ffn_step, 1)
                ffn_wait(p, 4)
                dve.sem_inc(hits_done, 1)

            def dense_part(p, quad, j):
                at = rows(quad, j, 1)
                dve.wait_ge(dense_mm, p * TPQ + j + 1)
                dve.wait_ge(bias_added, p * TPQ + j + 1)
                dve.scalar_tensor_tensor(selected[:, at], ps[:, dense_bank(p, j), :], selects(p)[:, j:j + 1], selected[:, at],
                                         ALU.mult, ALU.add).then_inc(dense_out, 1)

            def body(u, proj, attn, L=None, quad=None, source=None, p=None):
                for i in range(PROJ_OUTS):
                    if proj and i < PROJ_OUTS - 1:
                        proj_lo(u, i)
                    if attn and i < 4:
                        normalise(u - 1, i + 4)
                    if attn:
                        pT_lo_part(u, i)
                        if i in (1, 3, 4):
                            oT_lo_part(u, {1: 0, 3: 1, 4: 2}[i])
                    if L is not None:
                        t_u = u if attn else None
                        if i == 0:
                            if p is not None:
                                dve.wait_ge(added, u * QTILES)
                            ln_stats_of(L, source, 0)
                            ln_stats_of(L, source, 1)
                        elif i == 1:
                            ln_stats_of(L, source, 2)
                            ln_stats_of(L, source, 3)
                            ln_var(L)
                        elif i == 2:
                            ln_scale(L)
                            ln_apply(L, 0, source, t_u)
                        elif i == 3:
                            ln_apply(L, 1, source, t_u)
                            ln_apply(L, 2, source, t_u)
                            ln_apply(L, 3, source, t_u)
                        else:
                            ln_lo(L, 2 * i - 8, quad)
                            ln_lo(L, 2 * i - 7, quad)
                if attn:
                    oT_lo_part(u, 3)
                    add_out(u, 0)
                if proj:
                    add_bias(u, 0)
                    add_bias(u, 1)
                    dve.wait_ge(v_hi_done, u + 1)
                    dve.tensor_tensor(v_lo[:], ps[:, TR[0], :].rearrange("p (t d) -> p t d", t=TPQ),
                                      v_hi[:].bitcast(F32), ALU.subtract).then_inc(v_lo_done, 1)
                if attn:
                    add_out(u, 1)
                if p is not None:
                    cluster_bias(p)
                    cluster_hits(p)
                    dense_part(p, source, 0)
                if is_first(u):
                    for i in range(2, 6):
                        add_bias(u, i)
                    normalise(u, 0)
                    normalise(u, 1)
                    add_bias(u, 6)
                    add_bias(u, 7)
                    normalise(u, 2)
                    normalise(u, 3)
                    return
                if proj:
                    add_bias(u, 2)
                    add_bias(u, 3)
                    normalise(u, 0)
                    normalise(u, 1)
                if p is not None:
                    dense_part(p, source, 1)
                if attn:
                    add_out(u, 2)
                if proj:
                    add_bias(u, 4)
                    add_bias(u, 5)
                    normalise(u, 2)
                    normalise(u, 3)
                if p == 0:
                    dense_part(p, source, 2)
                if p == 0:
                    add_bias(u, 6)
                    add_bias(u, 7)
                if attn:
                    add_out(u, 3)
                if p == 0:
                    dense_part(p, source, 3)
                elif proj:
                    add_bias(u, 6)
                    add_bias(u, 7)

            dve.sem_inc(dense_out, TPQ)
            for j in range(TPQ):
                dve.wait_ge(tile_loaded[j], 16)
                ln_stats_of(0, 0, j)
            ln_var(0)
            ln_scale(0)
            for j in range(TPQ):
                ln_apply(0, j, 0)
            for j in range(TPQ):
                ln_lo(0, j, 0)
            dve.wait_ge(w_hi_done, NC)
            dve.tensor_tensor(wqkv_lo[:, NC - 1, :], first_raw(NC - 1), wqkv_hi[:, NC - 1, :].bitcast(F32),
                              ALU.subtract).then_inc(w_last_lo, 1)
            dve.wait_ge(ffn_consts, 3)
            dve.wait_ge(assign_loaded, 16)
            step(dve.tensor_copy(prob[0:CLUSTERS, 5, :], prob[0:CLUSTERS, 4, :].bitcast(I32)))
            dve.tensor_scalar(onehot[:], prob[0:CLUSTERS, 5, :], cluster_id[:], None, ALU.is_equal).then_inc(onehot_ready, 1)

            dve.wait_ge(dist_sqrt, 1)
            step(dve.reciprocal(bias[:, 1, :], bias[:, 0, :]))
            step(dve.tensor_tensor(bias[:, 2, :], bias[:, 1, :], dist[:], ALU.mult))
            step(dve.tensor_tensor(bias[:, 3, :], bias[:, 2, :], bias[:, 0, :], ALU.add))
            dve.tensor_scalar(dist[:], bias[:, 3, :], -0.5, None, ALU.mult).then_inc(dist_ready, 1)
            dve.wait_ge(x_loaded[1], 16)
            body(0, True, False, 1, 1, 1)
            dve.wait_ge(x_loaded[2], 16)
            dve.wait_ge(x_loaded[3], 16)
            with dve.Fori(1, QUADS - 1) as u:
                body(u, True, True, u + 1, u + 1, u + 1)
            with dve.Fori(QUADS - 1, UNITS - 2) as u:
                body(u, True, True)
            for t in range(NC):
                dve.wait_ge(wT_hi_done, t + 1)
                dve.tensor_tensor(wT_lo[:, :, t * P:(t + 1) * P], ps[:, WT_BANKS[t], :].rearrange("p (c t) -> p c t", c=NC),
                                  wT_hi[:, :, t * P:(t + 1) * P].bitcast(F32), ALU.subtract).then_inc(wT_lo_done, 1)
            dve.wait_ge(wT_hi_done, NC + 1)
            dve.tensor_tensor(cT[:, :, 1, :], ps[:, WT_BANKS[NC], 0:NC * CLUSTERS].rearrange("p (c n) -> p c n", c=NC),
                              cT[:, :, 0, :].bitcast(F32), ALU.subtract).then_inc(wT_lo_done, 1)
            dve.wait_ge(bias_loaded, 16)
            body(UNITS - 2, True, True, 4, 0, 0, 0)
            body(UNITS - 1, True, True, 5, 0, 1, 1)
            u = UNITS

            def finish(t, n):
                at = slice(t * HID, (t + n) * HID)
                mask = ps[:, MASK_BANK, :].bitcast(I32).rearrange("p (a n) -> p a n", a=1).broadcast_to([P, n, HID])
                dve.copy_predicated(acc[:, at].rearrange("p (t n) -> p t n", t=n), mask,
                                    selected[:, at].rearrange("p (t n) -> p t n", t=n)).then_inc(final, n)

            pT_lo_part(u, 0)
            pT_lo_part(u, 1)
            normalise(u - 1, 4)
            normalise(u - 1, 5)
            dve.wait_ge(added, u * QTILES)
            ln_stats_of(6, 2, 0)
            oT_lo_part(u, 0)
            ln_stats_of(6, 2, 1)
            pT_lo_part(u, 2)
            normalise(u - 1, 6)
            normalise(u - 1, 7)
            pT_lo_part(u, 3)
            ln_stats_of(6, 2, 2)
            oT_lo_part(u, 1)
            ln_stats_of(6, 2, 3)
            ln_var(6)
            dense_part(1, 1, 2)
            pT_lo_part(u, 4)
            oT_lo_part(u, 2)
            ln_scale(6)
            pT_lo_part(u, 5)
            dense_part(1, 1, 3)
            for j in range(TPQ):
                ln_apply(6, j, 2, u)

            def add_and_count(k):
                add_out(u, k)
                dve.wait_ge(added, u * QTILES + k + 1)
                ln_stats_of(7, 3, k)

            add_and_count(0)
            oT_lo_part(u, 3)
            add_and_count(1)
            for j in range(TPQ):
                ln_lo(6, j, 0)
            add_and_count(2)
            add_and_count(3)
            ln_var(7)
            ln_scale(7)
            for j in range(TPQ):
                ln_apply(7, j, 3)
            for j in range(TPQ):
                ln_lo(7, j, LAST)
            cluster_bias(2)
            cluster_hits(2)
            cluster_bias(3)
            dense_part(2, 2, 0)
            cluster_hits(3)
            dve.tensor_reduce(any_hit[:], quad_hits[:].rearrange("p (q c) -> p c q", c=CLUSTERS), AX_X,
                              ALU.max).then_inc(any_ready, 1)
            dve.wait_ge(sel_mm, 1)
            dve.tensor_scalar(cluster_sel[:], ps[0:CLUSTERS, PV[0], 0:P], 0.0, None, ALU.is_gt).then_inc(csel_ready, 1)
            dense_part(2, 2, 1)
            dve.wait_ge(sel_mm, 2)
            finish(0, 4)
            dense_part(2, 2, 2)
            dense_part(2, 2, 3)
            finish(4, 4)
            dense_part(3, 3, 0)
            dve.wait_ge(dense_out, TPQ * QUADS)
            finish(8, 4)
            dense_part(3, 3, 1)
            dense_part(3, 3, 2)
            dve.wait_ge(dense_out, TPQ * (QUADS + 1) - 1)
            finish(12, 2)
            finish(14, 1)
            dense_part(3, 3, 3)
            dve.wait_ge(dense_out, TPQ * (QUADS + 1))
            finish(15, 1)

        @block.tensor
        def _(pe):
            def three_pass(dst, terms, start, stop):
                n = 3 * len(terms)
                m = 0
                for (l_hi, l_lo), (r_hi, r_lo) in terms:
                    for l, r in ((l_hi, r_hi), (l_hi, r_lo), (l_lo, r_hi)):
                        ins = pe.matmul(dst, l, r, start=start and m == 0, stop=stop and m == n - 1)
                        m += 1
                return ins

            pe.sem_inc(pT_mm, CHUNKS)
            pe.sem_inc(pv_mm, QTILES)
            pe.sem_inc(wo_mm, QTILES)
            pe.wait_ge(ident_ready, 1)

            def keep_busy(n):
                for _ in range(n):
                    pe.transpose(ps[:, PJ[0], 0:P], ident[:], ident[:])

            keep_busy(36)

            def ln_transpose(L, j):
                pe.wait_ge(ln_ready, L * TPQ + j + 1)
                if not own_banks(L):
                    pe.wait_ge(ln_lo_done, L * TPQ + j - 1)
                for c in range(NC):
                    ins = pe.transpose(ps[:, ln_bank(L, j), c * P:(c + 1) * P], prob[:, j, c * P:(c + 1) * P], ident[:])
                ins.then_inc(ln_mm, 1)

            def project(u, i):
                first = is_first(u) and i == 0
                if i == 0 and not first:
                    pe.wait_ge(wqkv_ready, group_count(u))
                col = HPG * D if i == 0 else (HPG + 1) * D if i == PROJ_OUTS - 1 else (i - 1) * D
                flat = xnT[:].rearrange("p q s c t -> p (q s c t)")
                at = [quad_of(u) * (2 * NC * UT) + n * UT for n in range(2 * NC)]
                terms = [((wqkv_hi[:, c, col:col + D], wqkv_lo[:, c, col:col + D]),
                          (flat[:, bass.ds(at[c], UT)], flat[:, bass.ds(at[NC + c], UT)])) for c in range(NC)]
                for c in range(NC):
                    if first:
                        pe.wait_ge(*((raw_split, c + 1) if c < NC - 1 else (w_last_lo, 1)))
                    ins = three_pass(ps[:, PJ[i % 2], :], terms[c:c + 1], c == 0, c == NC - 1)
                ins.then_inc(qkv_mm, 1)

            def transpose_probs(u, c):
                b, qt, kt, blocks = chunk_blocks(c)
                pe.wait_ge(probs_ready, u * SCORE_BANKS - SCORE_BANKS + 4 * b + 2 * qt + 2)
                for h, (bank, col) in enumerate(blocks):
                    ins = pe.transpose(ps[:, TR[c % 2], h * P:(h + 1) * P], prob[:, bank, col:col + P], ident[:])
                ins.then_inc(pT_mm, 1)

            def apply_v(u, c):
                b, qt, kt, _ = chunk_blocks(c)
                k = 2 * b + qt
                pe.wait_ge(pT_lo_done, u * CHUNKS + c + 1)
                if kt == 0:
                    pe.wait_ge(oT_lo_done, u * QTILES + k - 1)
                t = 2 * b + kt
                ins = three_pass(ps[:, PV[k % 2], :], [((v_hi[:, t, :], v_lo[:, t, :]), (pT_hi[:, c % 2, :], pT_lo[:, c % 2, :]))],
                                 kt == 0, kt == qt)
                if kt == qt:
                    ins.then_inc(pv_mm, 1)

            def project_out(u, k):
                pe.wait_ge(oT_lo_done, u * QTILES + k + 1)
                terms = [((oT_hi[:, k % 3, h * P:(h + 1) * P], oT_lo[:, k % 3, h * P:(h + 1) * P]),
                          (wo_hi[:, h, :], wo_lo[:, h, :])) for h in range(HPG)]
                three_pass(ps[:, out_bank(u, k), :], terms, True, True).then_inc(wo_mm, 1)

            def scores(u, i):
                b, qt, heads = score_slices(i)
                if not is_first(u):
                    pe.wait_ge(scores_biased, u * SCORE_BANKS + i - 1)
                elif 0 < i < len(FIRST_SC):
                    pe.wait_ge(ln_lo_done, TPQ + i)
                elif i > 0:
                    pe.wait_ge(scores_biased, i - len(FIRST_SC) + 1)
                for h, col, _, _, _ in heads:
                    q0 = b * SEQ + qt * P
                    q_hi, q_lo = qT_hi[:, h, q0:q0 + P], qT_lo[:, h, q0:q0 + P]
                    dst = ps[:, score_bank(u, i), col:col + SEQ]
                    if qt == 0:
                        both = kT[:, 2 * b, :, :]
                        pe.matmul(dst, q_hi, both, start=True, stop=False)
                        ins = pe.matmul(dst, q_lo, both, start=False, stop=True)
                    else:
                        ins = three_pass(dst, [((q_hi, q_lo), (kT[:, 2 * b:2 * b + 2, 0, :], kT[:, 2 * b:2 * b + 2, 1, :]))],
                                         True, True)
                ins.then_inc(s_mm, 1)

            def cluster_logits(p, u):
                pe.wait_ge(ln_lo_done, p * TPQ + TPQ * (QUADS + 1))
                if u is not None:
                    pe.wait_ge(pT_lo_done, u * CHUNKS + CHUNKS)
                for c in range(NC):
                    for n, x in enumerate(ffn_x(p)):
                        ins = pe.matmul(ps[:, logit_bank(p), :], cT[:, c, :, :], x[:, c, :], start=c == n == 0,
                                        stop=c == NC - 1 and n == 1)
                ins.then_inc(logitT_mm, 1)

            def transpose_logits(p):
                pe.wait_ge(logitT_copied, p + 1)
                for j in range(TPQ):
                    ins = pe.matmul(ps[:, logit_bank(p), j * CLUSTERS:(j + 1) * CLUSTERS], logitT[:, j * P:(j + 1) * P], fold[:],
                                    start=True, stop=True)
                ins.then_inc(logit_mm, 1)

            def dense(p, j, chunks=range(NC)):
                at = slice(j * P, (j + 1) * P)
                n = p * TPQ + j
                if 0 in chunks and n < FFN_TAIL:
                    pe.wait_ge(dense_out, n + 3)
                elif 0 in chunks and p == QUADS - 1 and j < 2:
                    pe.wait_ge(dense_out, n + 1)
                x_hi, x_lo = ffn_x(p)
                for c in chunks:
                    term = ((x_hi[:, c, at], x_lo[:, c, at]), (wT_hi[:, c, :], wT_lo[:, c, :]))
                    ins = three_pass(ps[:, dense_bank(p, j), :], [term], c == 0, c == NC - 1)
                if NC - 1 in chunks:
                    ins.then_inc(dense_mm, 1)

            def body(u, proj, attn, L=None, p=None):
                for i in range(PROJ_OUTS):
                    if proj:
                        if i < 2:
                            if attn:
                                pe.wait_ge(added, u * QTILES + i - 1)
                        else:
                            pe.wait_ge(qk_lo_done, u * 5 + i - 1)
                        project(u, i)
                    if attn:
                        if i == 0:
                            pe.wait_ge(v_lo_done, u)
                        else:
                            pe.wait_ge(pT_lo_done, u * CHUNKS + i - 1)
                        if i == 1 and p is not None:
                            pe.wait_ge(wT_lo_done, NC + 1)
                            pe.wait_ge(cl_exp_done, p + 1)
                            pe.wait_ge(dense_out, p * TPQ + TPQ)
                        if i == 1 and L is not None:
                            pe.wait_ge(scores_biased, u * SCORE_BANKS)
                        transpose_probs(u, i)
                        if i > 0:
                            apply_v(u, i - 1)
                    if L is not None and i >= 4:
                        ln_transpose(L, 2 * i - 8)
                        ln_transpose(L, 2 * i - 7)
                if attn:
                    if proj:
                        pe.wait_ge(qk_lo_done, u * 5 + 5)
                    else:
                        pe.wait_ge(added, u * QTILES - 1)
                    pe.wait_ge(wo_ready, group_count(u - 1))
                    project_out(u, 0)
                    apply_v(u, CHUNKS - 1)
                if proj:
                    if not attn:
                        pe.wait_ge(qk_lo_done, 5)
                    if L is not None and attn:
                        pe.wait_ge(ln_lo_done, L * TPQ + TPQ)
                    scores(u, 0)
                    scores(u, 1)
                    pe.wait_ge(qkv_hi_done, u * PROJ_OUTS + 6)
                    pe.wait_ge(pT_lo_done, u * CHUNKS + 5)
                    for t in range(TPQ):
                        ins = pe.transpose(ps[:, TR[0], t * P:(t + 1) * P], vT[:, t * P:(t + 1) * P], ident[:])
                    ins.then_inc(v_mm, 1)
                if p is not None:
                    cluster_logits(p, u)
                if attn:
                    if not proj:
                        pe.wait_ge(added, u * QTILES)
                    project_out(u, 1)
                if p is not None:
                    transpose_logits(p)
                    pe.wait_ge(oT_lo_done, u * QTILES + QTILES)
                    dense(p, 0)
                if proj:
                    scores(u, 2)
                    scores(u, 3)
                if p is not None:
                    dense(p, 1)
                if attn:
                    pe.wait_ge(added, u * QTILES + 1)
                    project_out(u, 2)
                if proj:
                    scores(u, 4)
                    scores(u, 5)
                if p == 0:
                    dense(p, 2)
                if p == 0:
                    scores(u, 6)
                    scores(u, 7)
                if attn:
                    pe.wait_ge(added, u * QTILES + 2)
                    project_out(u, 3)
                if p == 0:
                    dense(p, 3)
                elif proj:
                    scores(u, 6)
                    scores(u, 7)

            for j in range(TPQ):
                ln_transpose(0, j)
            keep_busy(16)
            pe.wait_ge(ln_lo_done, TPQ)
            body(0, True, False, 1)
            with pe.Fori(1, QUADS - 1) as u:
                pe.wait_ge(ln_lo_done, u * TPQ + TPQ)
                body(u, True, True, u + 1)
            pe.wait_ge(ln_lo_done, TPQ * QUADS)
            with pe.Fori(QUADS - 1, UNITS - 2) as u:
                body(u, True, True)
            pe.wait_ge(ffn_consts, 3)
            pe.wait_ge(wc_loaded, 32)
            pe.wait_ge(oT_lo_done, QTILES * (UNITS - 2))
            pe.wait_ge(pT_lo_done, CHUNKS * (UNITS - 2))
            for t in range(NC):
                if t == NC - 1:
                    pe.wait_ge(scores_biased, SCORE_BANKS * (UNITS - 2))
                for c in range(NC):
                    ins = pe.transpose(ps[:, WT_BANKS[t], c * P:(c + 1) * P], w_raw[:, t, c * P:(c + 1) * P], ident[:])
                ins.then_inc(wT_mm, 1)
            for c in range(NC):
                ins = pe.transpose(ps[:, WT_BANKS[NC], c * CLUSTERS:(c + 1) * CLUSTERS], c_raw[:, c * P:(c + 1) * P],
                                   ident[0:CLUSTERS, 0:CLUSTERS])
            ins.then_inc(wT_mm, 1)
            body(UNITS - 2, True, True, 4, 0)
            body(UNITS - 1, True, True, 5, 1)
            u = UNITS
            pe.wait_ge(v_lo_done, u)
            transpose_probs(u, 0)
            pe.wait_ge(cl_exp_done, 3)
            transpose_probs(u, 1)
            pe.wait_ge(added, u * QTILES - 1)
            dense(1, 2)
            pe.wait_ge(dense_out, TPQ + FFN_TAIL)
            apply_v(u, 0)
            pe.wait_ge(pT_lo_done, u * CHUNKS + 1)
            transpose_probs(u, 2)
            apply_v(u, 1)
            pe.wait_ge(pT_lo_done, u * CHUNKS + 2)
            transpose_probs(u, 3)
            pe.wait_ge(scores_biased, u * SCORE_BANKS)
            dense(1, 3)
            apply_v(u, 2)
            pe.wait_ge(added, u * QTILES)
            pe.wait_ge(wo_ready, group_count(u - 1))
            project_out(u, 0)
            pe.wait_ge(pT_lo_done, u * CHUNKS + 3)
            transpose_probs(u, 4)
            apply_v(u, 3)
            pe.wait_ge(pT_lo_done, u * CHUNKS + 4)
            transpose_probs(u, 5)
            project_out(u, 1)
            apply_v(u, 4)
            apply_v(u, 5)
            pe.wait_ge(dense_out, TPQ + FFN_TAIL + 1)
            project_out(u, 2)
            pe.wait_ge(pT_lo_done, u * CHUNKS + CHUNKS)
            ln_transpose(6, 0)
            ln_transpose(6, 1)
            pe.wait_ge(oT_lo_done, u * QTILES + QTILES)
            ln_transpose(6, 2)
            ln_transpose(6, 3)
            pe.wait_ge(dense_out, TPQ + FFN_TAIL + 2)
            project_out(u, 3)
            cluster_logits(2, u)
            pe.wait_ge(added, u * QTILES + 2)
            dense(2, 0)
            transpose_logits(2)
            pe.wait_ge(added, u * QTILES + QTILES)
            for j in range(TPQ):
                ln_transpose(7, j)
            dense(2, 1)
            cluster_logits(3, None)
            dense(2, 2, (0, 1))
            transpose_logits(3)
            dense(2, 2, (2, 3))
            pe.wait_ge(cl_exp_done, 4)
            dense(2, 3)
            dense(3, 0, (0,))
            pe.wait_ge(any_ready, 1)
            pe.matmul(ps[0:CLUSTERS, PV[0], 0:P], any_hit[:], ones[:], start=True, stop=True).then_inc(sel_mm, 1)
            pe.wait_ge(csel_ready, 1)
            pe.wait_ge(onehot_ready, 1)
            pe.matmul(ps[:, MASK_BANK, :], cluster_sel[:], onehot[:], start=True, stop=True).then_inc(sel_mm, 1)
            dense(3, 0, (1, 2, 3))
            dense(3, 1)
            dense(3, 2)
            dense(3, 3)


_INS = ['L0_attn_hidden_states', 'L0_attn_w_qkv', 'L0_attn_w_o', 'L0_ffn_weight', 'L0_ffn_bias', 'L0_ffn_centroids',
        'L0_ffn_assignments']


def kernel(**inputs):
    import numpy as np
    import concourse.bacc as bacc
    from concourse.bass_utils import run_bass_kernel_spmd

    nc = bacc.Bacc("TRN2", target_bir_lowering=False, num_devices=1)
    arrays, args = {}, []
    for name in _INS:
        a = np.ascontiguousarray(inputs[name])
        if name == 'L0_attn_hidden_states':
            a = a.reshape(TOK, HID)
        arrays[f"in_{name}"] = a
        args.append(nc.dram_tensor(f"in_{name}", a.shape, mybir.dt.from_np(a.dtype), kind="ExternalInput").ap())
    args.append(nc.dram_tensor("out", [TOK, HID], F32, kind="ExternalOutput").ap())
    build(nc, *args)
    r = run_bass_kernel_spmd(nc, [arrays], core_ids=[0])
    return r.results[0]["out"].reshape(BATCH, SEQ, HID)
```
